# Optimizing a Trainium2 kernel written in Bass

```python
import numpy as np
import jax
import jax.numpy as jnp

def _softmax(x, axis=-1):
    return jax.nn.softmax(x, axis=axis)
def _gelu(x):
    return jax.nn.gelu(x, approximate=True)
def _silu(x):
    return jax.nn.silu(x)
def _sigmoid(x):
    return jax.nn.sigmoid(x)
def _layernorm(x, axis=-1, eps=1e-5):
    m = jnp.mean(x, axis=axis, keepdims=True)
    v = jnp.var(x, axis=axis, keepdims=True)
    return (x - m) / jnp.sqrt(v + eps)
def _scatter_add(tgt, idx, src, axis=0):
    return tgt.at[idx].add(src)
def _segment_sum(src, seg, n):
    return jax.ops.segment_sum(src, seg, n)

kernel_name = 'mk_conv_seq_d2_conv_nhwc192_b73fcd'

def setup_inputs(seed: int = 0):
    np.random.seed(seed)
    _w = jnp.asarray
    def _rec_inputs():
        import jax
        import jax.numpy as jnp
        _gk = jax.random.key(seed)
        x = 7.572e-06 + 1 * jax.random.normal(jax.random.fold_in(_gk, 1), (16, 56, 56, 192), jnp.float32)
        return x
    x = _rec_inputs()
    def _L0_conv_setup():
        import jax, jax.numpy as jnp
        import numpy as np
        WS = 7
        SHIFT = 3
        NH = 6

        def layernorm(x, w, b, eps=1e-05):
            mu = jnp.mean(x, axis=-1, keepdims=True)
            var = jnp.var(x, axis=-1, keepdims=True)
            return (x - mu) * jax.lax.rsqrt(var + eps) * w + b
        key = jax.random.key(seed)
        ks = jax.random.split(key, 8)
        B, H, W, C = (16, 56, 56, 192)
        hid = 4 * C
        s = lambda k, shape, fan: jax.random.normal(k, shape, jnp.float32) * fan ** (-0.5)
        return {'x': jax.random.normal(ks[0], (B, H, W, C), jnp.float32), 'ln1_w': jnp.ones((C,), jnp.float32), 'ln1_b': jnp.zeros((C,), jnp.float32), 'qkv_w': s(ks[1], (C, 3 * C), C), 'qkv_b': jnp.zeros((3 * C,), jnp.float32), 'proj_w': s(ks[2], (C, C), C), 'proj_b': jnp.zeros((C,), jnp.float32), 'ln2_w': jnp.ones((C,), jnp.float32), 'ln2_b': jnp.zeros((C,), jnp.float32), 'mlp_w1': s(ks[3], (C, hid), C), 'mlp_b1': jnp.zeros((hid,), jnp.float32), 'mlp_w2': s(ks[4], (hid, C), hid), 'mlp_b2': jnp.zeros((C,), jnp.float32)}
    _L0_conv_all = _L0_conv_setup()
    _L0_conv_in = {k: v for k, v in _L0_conv_all.items() if k in ('ln1_w', 'ln1_b', 'qkv_w', 'qkv_b', 'proj_w', 'proj_b', 'ln2_w', 'ln2_b', 'mlp_w1', 'mlp_b1', 'mlp_w2', 'mlp_b2', )}
    del _L0_conv_all

    def _L1_conv_setup():
        import jax, jax.numpy as jnp
        import numpy as np
        B_SZ, H_DIM, W_DIM, D_MODEL = (2, 64, 64, 192)
        N_STATE = 16
        R_RANK = 12
        K_DIRS = 4
        LN_EPS = 1e-05

        def _cross_scan(x):
            b, d, h, w = x.shape
            x0 = x.reshape(b, d, h * w)
            x1 = jnp.transpose(x, (0, 1, 3, 2)).reshape(b, d, h * w)
            xs = jnp.stack([x0, x1], axis=1)
            return jnp.concatenate([xs, jnp.flip(xs, axis=-1)], axis=1)

        def _cross_merge(ys, h, w):
            b, _, d, l = ys.shape
            ys = ys[:, 0:2] + jnp.flip(ys[:, 2:4], axis=-1)
            y1 = jnp.transpose(ys[:, 1].reshape(b, d, w, h), (0, 1, 3, 2)).reshape(b, d, l)
            return ys[:, 0] + y1

        def _selective_scan(xs, dts, A, Bs, Cs):
            b, k, d, l = xs.shape
            n = A.shape[-1]

            @jax.checkpoint
            def step(h_prev, t):
                x_t, dt_t, B_t, C_t = t
                dA = jnp.exp(dt_t[..., None] * A)
                dBx = (dt_t * x_t)[..., None] * B_t[:, :, None, :]
                h = dA * h_prev + dBx
                y = jnp.einsum('bkdn,bkn->bkd', h, C_t)
                return (h, y)
            seq = (jnp.moveaxis(xs, -1, 0), jnp.moveaxis(dts, -1, 0), jnp.moveaxis(Bs, -1, 0), jnp.moveaxis(Cs, -1, 0))
            h0 = jnp.zeros((b, k, d, n), xs.dtype)
            _, ys = jax.lax.scan(step, h0, seq)
            return jnp.moveaxis(ys, 0, -1)
        key = jax.random.key(seed)
        ks = jax.random.split(key, 5)
        x = jax.random.normal(ks[0], (B_SZ, H_DIM, W_DIM, D_MODEL), jnp.float32)
        x_proj_weight = jax.random.normal(ks[1], (K_DIRS, R_RANK + 2 * N_STATE, D_MODEL), jnp.float32) * 0.02
        dt_projs_weight = jax.random.uniform(ks[2], (K_DIRS, D_MODEL, R_RANK), jnp.float32, -R_RANK ** (-0.5), R_RANK ** (-0.5))
        dt = jnp.exp(jax.random.uniform(ks[3], (K_DIRS, D_MODEL)) * (np.log(0.1) - np.log(0.001)) + np.log(0.001))
        dt = jnp.clip(dt, 0.0001, None)
        dt_projs_bias = dt + jnp.log(-jnp.expm1(-dt))
        A_logs = jnp.log(jnp.tile(jnp.arange(1, N_STATE + 1, dtype=jnp.float32), (K_DIRS * D_MODEL, 1)))
        Ds = jnp.ones((K_DIRS * D_MODEL,), jnp.float32)
        ln_weight = jnp.ones((D_MODEL,), jnp.float32)
        ln_bias = jnp.zeros((D_MODEL,), jnp.float32)
        return dict(x=x, x_proj_weight=x_proj_weight, dt_projs_weight=dt_projs_weight, dt_projs_bias=dt_projs_bias, A_logs=A_logs, Ds=Ds, ln_weight=ln_weight, ln_bias=ln_bias)
    _L1_conv_all = _L1_conv_setup()
    _L1_conv_in = {k: v for k, v in _L1_conv_all.items() if k in ('x_proj_weight', 'dt_projs_weight', 'dt_projs_bias', 'A_logs', 'Ds', 'ln_weight', 'ln_bias', )}
    del _L1_conv_all

    return {
        "x": x,
        "L0_conv_ln1_w": _L0_conv_in["ln1_w"],
        "L0_conv_ln1_b": _L0_conv_in["ln1_b"],
        "L0_conv_qkv_w": _L0_conv_in["qkv_w"],
        "L0_conv_qkv_b": _L0_conv_in["qkv_b"],
        "L0_conv_proj_w": _L0_conv_in["proj_w"],
        "L0_conv_proj_b": _L0_conv_in["proj_b"],
        "L0_conv_ln2_w": _L0_conv_in["ln2_w"],
        "L0_conv_ln2_b": _L0_conv_in["ln2_b"],
        "L0_conv_mlp_w1": _L0_conv_in["mlp_w1"],
        "L0_conv_mlp_b1": _L0_conv_in["mlp_b1"],
        "L0_conv_mlp_w2": _L0_conv_in["mlp_w2"],
        "L0_conv_mlp_b2": _L0_conv_in["mlp_b2"],
        "L1_conv_x_proj_weight": _L1_conv_in["x_proj_weight"],
        "L1_conv_dt_projs_weight": _L1_conv_in["dt_projs_weight"],
        "L1_conv_dt_projs_bias": _L1_conv_in["dt_projs_bias"],
        "L1_conv_A_logs": _L1_conv_in["A_logs"],
        "L1_conv_Ds": _L1_conv_in["Ds"],
        "L1_conv_ln_weight": _L1_conv_in["ln_weight"],
        "L1_conv_ln_bias": _L1_conv_in["ln_bias"],
    }

def reference(x, L0_conv_ln1_w, L0_conv_ln1_b, L0_conv_qkv_w, L0_conv_qkv_b, L0_conv_proj_w, L0_conv_proj_b, L0_conv_ln2_w, L0_conv_ln2_b, L0_conv_mlp_w1, L0_conv_mlp_b1, L0_conv_mlp_w2, L0_conv_mlp_b2, L1_conv_x_proj_weight, L1_conv_dt_projs_weight, L1_conv_dt_projs_bias, L1_conv_A_logs, L1_conv_Ds, L1_conv_ln_weight, L1_conv_ln_bias):
    import jax
    import jax.numpy as jnp
    def _L0_conv_ref(x, ln1_w, ln1_b, qkv_w, qkv_b, proj_w, proj_b, ln2_w, ln2_b, mlp_w1, mlp_b1, mlp_w2, mlp_b2):
        import jax, jax.numpy as jnp
        import numpy as np
        WS = 7
        SHIFT = 3
        NH = 6

        def layernorm(x, w, b, eps=1e-05):
            mu = jnp.mean(x, axis=-1, keepdims=True)
            var = jnp.var(x, axis=-1, keepdims=True)
            return (x - mu) * jax.lax.rsqrt(var + eps) * w + b
        B, H, W, C = x.shape
        hd = C // NH
        scale = hd ** (-0.5)
        N = WS * WS
        shortcut = x
        xn = layernorm(x, ln1_w, ln1_b)
        xs = jnp.roll(xn, shift=(-SHIFT, -SHIFT), axis=(1, 2))
        xw = xs.reshape(B, H // WS, WS, W // WS, WS, C)
        xw = xw.transpose(0, 1, 3, 2, 4, 5).reshape(-1, N, C)
        qkv = xw @ qkv_w + qkv_b
        qkv = qkv.reshape(-1, N, 3, NH, hd).transpose(2, 0, 3, 1, 4)
        q, k, v = (qkv[0], qkv[1], qkv[2])
        attn = jnp.einsum('bhqd,bhkd->bhqk', q, k) * scale
        attn = jax.nn.softmax(attn, axis=-1)
        o = jnp.einsum('bhqk,bhkd->bhqd', attn, v)
        o = o.transpose(0, 2, 1, 3).reshape(-1, N, C)
        o = o @ proj_w + proj_b
        o = o.reshape(B, H // WS, W // WS, WS, WS, C)
        o = o.transpose(0, 1, 3, 2, 4, 5).reshape(B, H, W, C)
        o = jnp.roll(o, shift=(SHIFT, SHIFT), axis=(1, 2))
        x = shortcut + o
        h = layernorm(x, ln2_w, ln2_b)
        h = jax.nn.gelu(h @ mlp_w1 + mlp_b1, approximate=False)
        x = x + (h @ mlp_w2 + mlp_b2)
        return x

    def _L1_conv_ref(x, x_proj_weight, dt_projs_weight, dt_projs_bias, A_logs, Ds, ln_weight, ln_bias):
        import jax, jax.numpy as jnp
        import numpy as np
        B_SZ, H_DIM, W_DIM, D_MODEL = (2, 64, 64, 192)
        N_STATE = 16
        R_RANK = 12
        K_DIRS = 4
        LN_EPS = 1e-05

        def _cross_scan(x):
            b, d, h, w = x.shape
            x0 = x.reshape(b, d, h * w)
            x1 = jnp.transpose(x, (0, 1, 3, 2)).reshape(b, d, h * w)
            xs = jnp.stack([x0, x1], axis=1)
            return jnp.concatenate([xs, jnp.flip(xs, axis=-1)], axis=1)

        def _cross_merge(ys, h, w):
            b, _, d, l = ys.shape
            ys = ys[:, 0:2] + jnp.flip(ys[:, 2:4], axis=-1)
            y1 = jnp.transpose(ys[:, 1].reshape(b, d, w, h), (0, 1, 3, 2)).reshape(b, d, l)
            return ys[:, 0] + y1

        def _selective_scan(xs, dts, A, Bs, Cs):
            b, k, d, l = xs.shape
            n = A.shape[-1]

            @jax.checkpoint
            def step(h_prev, t):
                x_t, dt_t, B_t, C_t = t
                dA = jnp.exp(dt_t[..., None] * A)
                dBx = (dt_t * x_t)[..., None] * B_t[:, :, None, :]
                h = dA * h_prev + dBx
                y = jnp.einsum('bkdn,bkn->bkd', h, C_t)
                return (h, y)
            seq = (jnp.moveaxis(xs, -1, 0), jnp.moveaxis(dts, -1, 0), jnp.moveaxis(Bs, -1, 0), jnp.moveaxis(Cs, -1, 0))
            h0 = jnp.zeros((b, k, d, n), xs.dtype)
            _, ys = jax.lax.scan(step, h0, seq)
            return jnp.moveaxis(ys, 0, -1)
        b, h, w, d = x.shape
        l = h * w
        xc = jnp.transpose(x, (0, 3, 1, 2))
        xs = _cross_scan(xc)
        x_dbl = jnp.einsum('bkdl,kcd->bkcl', xs, x_proj_weight)
        dts, Bs, Cs = jnp.split(x_dbl, [R_RANK, R_RANK + N_STATE], axis=2)
        dts = jnp.einsum('bkrl,kdr->bkdl', dts, dt_projs_weight)
        dts = jax.nn.softplus(dts + dt_projs_bias[None, :, :, None])
        A = -jnp.exp(A_logs).reshape(K_DIRS, d, N_STATE)
        ys = _selective_scan(xs, dts, A, Bs, Cs)
        ys = ys + Ds.reshape(1, K_DIRS, d, 1) * xs
        y = _cross_merge(ys, h, w)
        y = jnp.transpose(y, (0, 2, 1))
        mu = jnp.mean(y, -1, keepdims=True)
        var = jnp.mean(jnp.square(y - mu), -1, keepdims=True)
        y = (y - mu) * jax.lax.rsqrt(var + LN_EPS) * ln_weight + ln_bias
        return y.reshape(b, h, w, d)

    def _gn(v, G=32, eps=1e-5):
        B_, H_, W_, C_ = v.shape
        g = v.reshape(B_, H_, W_, G, C_ // G)
        m = jnp.mean(g, axis=(1, 2, 4), keepdims=True)
        s = jnp.var(g, axis=(1, 2, 4), keepdims=True)
        return ((g - m) / jnp.sqrt(s + eps)).reshape(v.shape)

    def _ln_c(v, eps=1e-6):
        m = jnp.mean(v, axis=-1, keepdims=True)
        s = jnp.var(v, axis=-1, keepdims=True)
        return (v - m) / jnp.sqrt(s + eps)

    def _ln_t(v, eps=1e-5):
        m = jnp.mean(v, axis=-1, keepdims=True)
        s = jnp.var(v, axis=-1, keepdims=True)
        return (v - m) / jnp.sqrt(s + eps)

    def _to_tokens(v):
        B_, H_, W_, C_ = v.shape
        return v.reshape(B_, H_ * W_, C_)
    def _from_tokens(t, like):
        return t.reshape(like.shape)

    x = _L0_conv_ref(x, L0_conv_ln1_w, L0_conv_ln1_b, L0_conv_qkv_w, L0_conv_qkv_b, L0_conv_proj_w, L0_conv_proj_b, L0_conv_ln2_w, L0_conv_ln2_b, L0_conv_mlp_w1, L0_conv_mlp_b1, L0_conv_mlp_w2, L0_conv_mlp_b2)
    x = _L1_conv_ref(x, L1_conv_x_proj_weight, L1_conv_dt_projs_weight, L1_conv_dt_projs_bias, L1_conv_A_logs, L1_conv_Ds, L1_conv_ln_weight, L1_conv_ln_bias)
    return x


_drawn_inputs = setup_inputs


def setup_inputs(seed=0):
    import zlib

    import numpy as np

    out = dict(_drawn_inputs(seed))
    spreads = {'L0_conv_ln1_w': (1.0, 0.2),
     'L0_conv_ln1_b': (0.0, 0.1),
     'L0_conv_qkv_b': (0.0, 0.1),
     'L0_conv_proj_b': (0.0, 0.1),
     'L0_conv_ln2_w': (1.0, 0.2),
     'L0_conv_ln2_b': (0.0, 0.1),
     'L0_conv_mlp_b1': (0.0, 0.1),
     'L0_conv_mlp_b2': (0.0, 0.1),
     'L1_conv_Ds': (1.0, 0.2),
     'L1_conv_ln_weight': (1.0, 0.2),
     'L1_conv_ln_bias': (0.0, 0.1)}
    factors = {'L1_conv_x_proj_weight': 3.577,
     'L1_conv_dt_projs_weight': 8.0,
     'L1_conv_dt_projs_bias': 6.261,
     'L1_conv_A_logs': 7.316}
    for name, (base, spread) in spreads.items():
        noise = np.random.default_rng([zlib.crc32(name.encode()), seed]).standard_normal(out[name].shape)
        drawn = base * np.exp(spread * noise) if base else spread * noise
        out[name] = jnp.asarray(drawn.astype(out[name].dtype))
    for name, factor in factors.items():
        out[name] = (out[name] * factor).astype(out[name].dtype)
    return out
```

```python
from contextlib import ExitStack

import concourse.bass as bass
from concourse import mybir

ALU = mybir.AluOpType
ACT = mybir.ActivationFunctionType
AX_X = mybir.AxisListType.X
F32 = mybir.dt.float32
BF16 = mybir.dt.bfloat16

C = 192
HC = C // 2
IMG = 56
L = IMG * IMG
WS, SHIFT, NH = 7, 3, 6
HD = C // NH
WT = WS * WS
UW = IMG // WS
UT = UW * WT
PT = 2 * WT
NPAIR = UW // 2
HID = 4 * C
MC = HID // 128
SCALE = HD ** -0.5
LN_EPS = 1e-5

NS = 16
RANK = 12
LN_EXP = "natural_log_exp_and_others"
CH = 784
NCH = L // CH
DG = 8
NG = C // DG
NQ = C // 32
WPK = 2 * (C + 256) + 2

TT = 2 * IMG
NT = L // TT
GT = 4


def hold(eng, sem, value, fence):
    eng.wait_ge(sem, value)
    eng.sem_inc(fence, 1)


def build_layer0(nc, io, scr_a, n_units):
    x_win, w_qkv, w_proj, w1, w2, cols0, b1c, pb, ident = io
    with ExitStack() as ctx:
        sb = lambda name, shape, dt=F32: ctx.enter_context(nc.sbuf_tensor("a_" + name, shape, dt))
        sem = lambda name: ctx.enter_context(nc.semaphore(name))
        ps = ctx.enter_context(nc.psum_tensor("a_psum", [128, 8, 512], F32))

        wqkv_sb = sb("wqkv_sb", [HC, 2, 3 * C])
        wp_sb = sb("wp_sb", [HC, 2, C])
        w1_sb = sb("w1_sb", [HC, 2, HID])
        w2_sb = sb("w2_sb", [128, MC, C])
        cols = sb("cols", [HC, 16])
        b1_sb = sb("b1_sb", [128, MC])
        pb_sb = sb("pb_sb", [PT, C])
        id_sb = sb("id_sb", [128, 128])
        eps_sb = sb("eps_sb", [128, 1])
        x_sb = sb("x_sb", [PT, 2, NPAIR, C])
        xpb = sb("xpb", [PT, NPAIR, C])
        stats = sb("stats", [PT, 2, NPAIR, 6])
        mv = sb("mv", [PT, 2, NPAIR, 2])
        lnv = sb("lnv", [PT, 2, NPAIR])
        rstd = sb("rstd", [PT, 2, NPAIR])
        xhat = sb("xhat", [PT, 2, NPAIR, C])
        xnT = sb("xnT", [HC, 2, UT])
        qkT = sb("qkT", [HC, 4, UT])
        v_sb = sb("v_sb", [WT, UW, C])
        prob = sb("prob", [128, NPAIR, 3, 2, WT])
        mx = sb("mx", [128, NPAIR, 3, 2])
        sm = sb("sm", [128, NPAIR, 3, 2])
        rs = sb("rs", [128, NPAIR, 3, 2])
        pT = sb("pT", [WT, 2, 2, 3, 128])
        oT = sb("oT", [HC, 2, UT])
        x2 = sb("x2", [PT, NPAIR, C])
        h2T = sb("h2T", [HC, 2, UT])
        g_sb = sb("g_sb", [128, MC, UT])
        x1T = sb("x1T", [HC, 2, 2, UT])

        scores = lambda q: ps[:, 3 * (q % 2):3 * (q % 2) + 3, 0:2 * WT].rearrange("p r (a k) -> p r a k", a=2)
        score_rows = lambda q, w, r, hh: ps[64 * w:64 * w + WT, 3 * (q % 2) + r, WT * hh:WT * hh + WT]
        LN1W, LN1B, QKB, VB, LN2W, LN2B, B2 = 0, 2, 4, 8, 10, 12, 14

        w_in = sem("a_w_in")
        x_in = [sem("a_x_in0"), sem("a_x_in1")]
        x1_out = [sem("a_x1_out0"), sem("a_x1_out1")]
        ready = sem("a_ready")
        xpb_done = sem("a_xpb_done")
        ln_dve = [sem("a_ln1_dve"), sem("a_ln2_dve")]
        ln_act = [sem("a_ln1_act"), sem("a_ln2_act")]
        t1_done, t2_done = sem("a_t1_done"), sem("a_t2_done")
        xn_done, h2_done = sem("a_xn_done"), sem("a_h2_done")
        qk_full, qk_evac = sem("a_qk_full"), sem("a_qk_evac")
        v_full, v_evac = sem("a_v_full"), sem("a_v_evac")
        s_full = sem("a_s_full")
        max_done, sub_done, exp_done = sem("a_max"), sem("a_sub"), sem("a_exp")
        sum_done, rec_done, prob_done = sem("a_sum"), sem("a_rec"), sem("a_prob")
        pt_full, pt_evac = sem("a_pt_full"), sem("a_pt_evac")
        av_full, av_evac = sem("a_av_full"), sem("a_av_evac")
        pj_full, x2_done = sem("a_pj_full"), sem("a_x2_done")
        h_full, gelu_done = sem("a_h_full"), sem("a_gelu")
        m2_full, x1_done = sem("a_m2_full"), sem("a_x1_done")

        def units(eng, step, last):
            step(0, 0, 0, True, n_units == 1)
            with eng.Fori(0, n_units // 2 - 1) as i:
                step(2 * i + 1, i, 1, False, False)
                step(2 * i + 2, i + 1, 0, False, False)
            step(n_units - 1, n_units // 2 - 1, 1, False, True)
            last(n_units, n_units // 2, 0)

        fence = sem("layer0_fence")
        block = ctx.enter_context(nc.Block())

        @block.sync
        def _(sp):
            for dst, src in ((wqkv_sb[:], w_qkv.rearrange("(a p) n -> p a n", a=2)),
                             (wp_sb[:], w_proj.rearrange("(a p) n -> p a n", a=2)),
                             (w1_sb[:], w1.rearrange("(a p) n -> p a n", a=2)),
                             (w2_sb[:], w2.rearrange("(a p) n -> p a n", a=MC)),
                             (cols[:], cols0), (b1_sb[:], b1c), (id_sb[:], ident),
                             (pb_sb[:], pb.unsqueeze(0).to_broadcast([PT, C]))):
                sp.dma_start(dst, src).then_inc(w_in, 16)

            def load(u, par):
                src = x_win[bass.ds(u * UT, UT), :].rearrange("(t p) c -> p t c", p=PT)
                sp.dma_start(x_sb[:, par], src).then_inc(x_in[par], 16)

            def store(u, par):
                dst = scr_a[bass.ds(u, 1)].rearrange("u (a p) t -> p (u a) t", a=2)
                sp.dma_start(dst, x1T[:, par]).then_inc(x1_out[par], 16)

            sp.sem_inc(x1_out[0], 16)
            sp.sem_inc(x1_out[1], 16)
            load(0, 0)

            def step(u, half, par, first, is_last):
                if not is_last:
                    if not first:
                        sp.wait_ge(ln_dve[0], 3 * u)
                        sp.wait_ge(xpb_done, u)
                    load(u + 1, 1 - par)
                if not first:
                    sp.wait_ge(x1_done, 2 * u + 2)
                    store(u - 1, 1 - par)

            def last(u, half, par):
                sp.wait_ge(x1_done, 2 * u + 2)
                store(u - 1, 1 - par)
                sp.wait_ge(x1_out[0], 16 * half + 16)
                sp.wait_ge(x1_out[1], 16 * half + 16)

            units(sp, step, last)

        @block.gpsimd
        def _(pool):
            pool.wait_ge(w_in, 16 * 8)

            def step(u, half, par, first, is_last):
                pool.wait_ge(x_in[par], 16 * half + 16)
                if not first:
                    pool.wait_ge(x2_done, 2 * u)
                nc.gpsimd.tensor_tensor(xpb[:], x_sb[:, par], pb_sb[:].unsqueeze(1).to_broadcast([PT, NPAIR, C]),
                                        ALU.add).then_inc(xpb_done, 1)

            units(pool, step, lambda *a: None)

        @block.vector
        def _(dve):
            nc.vector.memset(ps[:, 0:6, :], 0.0)
            nc.vector.memset(eps_sb[:], LN_EPS).then_inc(ready, 1)

            def norm(which, u, src):
                for t in range(NPAIR):
                    ins = nc.vector.bn_stats(stats[:, which, t, :], src[:, t, :])
                ins.then_inc(ln_dve[which], 1)
                hold(dve, ln_dve[which], 3 * u + 1, fence)
                for t in range(NPAIR):
                    ins = nc.vector.bn_aggr(mv[:, which, t, :], stats[:, which, t, :])
                ins.then_inc(ln_dve[which], 1)
                dve.wait_ge(ln_act[which], 2 * u + 2)
                dve.wait_ge(ln_dve[which], 3 * u + 2)
                for t in range(NPAIR):
                    ins = nc.vector.tensor_scalar(xhat[:, which, t, :], src[:, t, :], mv[:, which, t, 0:1],
                                                  rstd[:, which, t:t + 1], ALU.subtract, ALU.mult)
                ins.then_inc(ln_dve[which], 1)

            def norm1(u, half, par):
                dve.wait_ge(x_in[par], 16 * half + 16)
                if not (isinstance(u, int) and u == 0):
                    dve.wait_ge(t1_done, u)
                norm(0, u, x_sb[:, par])

            def front(u, q):
                n = NPAIR * u + q
                dve.wait_ge(s_full, n + 1)
                nc.vector.tensor_reduce(mx[:, q], scores(q), AX_X, ALU.max).then_inc(max_done, 1)
                dve.wait_ge(max_done, n + 1)
                nc.vector.tensor_tensor(prob[:, q], scores(q), mx[:, q].unsqueeze(3).to_broadcast([128, 3, 2, WT]),
                                        ALU.subtract).then_inc(sub_done, 1)

            def back(u, q):
                n = NPAIR * u + q
                dve.wait_ge(exp_done, n + 1)
                nc.vector.tensor_reduce(sm[:, q], prob[:, q], AX_X, ALU.add).then_inc(sum_done, 1)
                dve.wait_ge(sum_done, n + 1)
                nc.vector.reciprocal(rs[:, q], sm[:, q]).then_inc(rec_done, 1)
                dve.wait_ge(rec_done, n + 1)
                nc.vector.tensor_tensor(prob[:, q], prob[:, q], rs[:, q].unsqueeze(3).to_broadcast([128, 3, 2, WT]),
                                        ALU.mult).then_inc(prob_done, 1)

            norm1(0, 0, 0)

            def step(u, half, par, first, is_last):
                if not first:
                    dve.wait_ge(t2_done, u)
                    dve.wait_ge(x2_done, 2 * u)
                    norm(1, u - 1, x2[:])
                for e in range(UW // 2):
                    dve.wait_ge(v_full, UW // 2 * u + e + 1)
                    if e == 0 and not first:
                        dve.wait_ge(av_full, u)
                    nc.vector.tensor_copy(v_sb[:, 2 * e:2 * e + 2, :], ps[0:WT, 6 + e % 2, 0:2 * C].rearrange(
                        "p (w c) -> p w c", w=2)).then_inc(v_evac, 1)
                if not first:
                    dve.wait_ge(pt_full, NPAIR * u)
                front(u, 0)
                for q in range(1, NPAIR):
                    front(u, q)
                    back(u, q - 1)
                back(u, NPAIR - 1)
                if not is_last:
                    norm1(u + 1, half + par, 1 - par)
                for q in range(NPAIR):
                    n = NPAIR * u + q
                    dve.wait_ge(pt_full, n + 1)
                    nc.vector.tensor_copy(pT[:, q % 2, 0], ps[0:WT, 2, 0:384].rearrange("p (r k) -> p r k", r=3))
                    nc.vector.tensor_copy(pT[:, q % 2, 1], ps[0:WT, 3, 0:384].rearrange("p (r k) -> p r k", r=3)
                                          ).then_inc(pt_evac, 1)
                if not first:
                    dve.wait_ge(m2_full, 2 * u)
                dve.wait_ge(xpb_done, u + 1)
                for e in range(2):
                    dve.wait_ge(pj_full, 2 * u + e + 1)
                    nc.vector.tensor_tensor(x2[:, 2 * e:2 * e + 2, :], xpb[:, 2 * e:2 * e + 2, :],
                                            ps[0:PT, 6 + e, 0:2 * C].rearrange("p (t c) -> p t c", t=2),
                                            ALU.add).then_inc(x2_done, 1)

            def last(u, half, par):
                dve.wait_ge(t2_done, u)
                dve.wait_ge(x2_done, 2 * u)
                norm(1, u - 1, x2[:])

            units(dve, step, last)

        @block.scalar
        def _(act):
            act.wait_ge(w_in, 16 * 8)
            act.wait_ge(ready, 1)

            def rstd_of(which, u):
                act.wait_ge(ln_dve[which], 3 * u + 2)
                nc.scalar.activation(lnv[:, which, :], mv[:, which, :, 1], ACT.Ln,
                                     bias=eps_sb[0:PT, :]).then_inc(ln_act[which], 1)
                act.wait_ge(ln_act[which], 2 * u + 1)
                nc.scalar.activation(rstd[:, which, :], lnv[:, which, :], ACT.Exp,
                                     scale=-0.5).then_inc(ln_act[which], 1)

            def affine(dst, wcol, bcol, done):
                for a in range(2):
                    ins = nc.scalar.activation(dst[:, a, :], ps[0:HC, a, 0:UT], ACT.Identity,
                                               bias=cols[:, bcol + a:bcol + a + 1], scale=cols[:, wcol + a:wcol + a + 1])
                ins.then_inc(done, 1)

            def mlp(u, par):
                act.wait_ge(t2_done, u + 2)
                affine(h2T, LN2W, LN2B, h2_done)

            def mlp_tail(u, half, par):
                for m in range(MC):
                    act.wait_ge(h_full, MC * u + m + 1)
                    nc.scalar.activation(g_sb[:, m, :], ps[:, 6 + m % 2, 0:UT], ACT.Gelu,
                                         bias=b1_sb[:, m:m + 1]).then_inc(gelu_done, 1)
                nc.scalar.preload_act_table_set(LN_EXP)
                for a in range(2):
                    act.wait_ge(m2_full, 2 * u + a + 1)
                    if a == 0:
                        act.wait_ge(x1_out[par], 16 * half + 16)
                    nc.scalar.activation(x1T[:, par, a, :].rearrange("p (i w j) -> p w i j", i=WS, w=UW),
                                         ps[0:HC, 4 + a, 0:UT].rearrange("p (w i j) -> p w i j", w=UW, i=WS),
                                         ACT.Identity, bias=cols[:, B2 + a:B2 + a + 1]).then_inc(x1_done, 1)

            act.sem_inc(x1_done, 2)
            nc.scalar.preload_act_table_set(LN_EXP)
            rstd_of(0, 0)

            def step(u, half, par, first, is_last):
                if not first:
                    rstd_of(1, u - 1)
                act.wait_ge(t1_done, u + 1)
                if not first:
                    act.wait_ge(v_full, UW // 2 * u)
                affine(xnT, LN1W, LN1B, xn_done)
                for e in range(4):
                    act.wait_ge(qk_full, 4 * u + e + 1)
                    if e == 0 and not first:
                        act.wait_ge(s_full, NPAIR * u)
                    nc.scalar.activation(qkT[:, e, :], ps[0:HC, 6 + e % 2, 0:UT], ACT.Identity,
                                         bias=cols[:, QKB + e:QKB + e + 1]).then_inc(qk_evac, 1)
                for q in range(NPAIR):
                    act.wait_ge(sub_done, NPAIR * u + q + 1)
                    nc.scalar.activation(prob[:, q], prob[:, q], ACT.Exp, scale=SCALE).then_inc(exp_done, 1)
                if not is_last:
                    rstd_of(0, u + 1)
                if not first:
                    mlp(u - 1, 1 - par)
                    mlp_tail(u - 1, half - (1 - par), 1 - par)
                act.wait_ge(av_full, u + 1)
                if not first:
                    act.wait_ge(pj_full, 2 * u)
                for a in range(2):
                    ins = nc.scalar.activation(oT[:, a, :], ps[0:HC, a, 0:UT], ACT.Identity,
                                               bias=cols[:, VB + a:VB + a + 1])
                ins.then_inc(av_evac, 1)

            def last(u, half, par):
                rstd_of(1, u - 1)
                mlp(u - 1, 1)
                mlp_tail(u - 1, half - 1, 1)

            units(act, step, last)

        @block.tensor
        def _(pe):
            pe.wait_ge(w_in, 16 * 8)
            pe.wait_ge(ready, 1)
            pe.sem_inc(t2_done, 1)

            def transposes(which, done):
                for t in range(NPAIR):
                    for a in range(2):
                        mm = pe.transpose(ps[0:HC, a, PT * t:PT * t + PT], xhat[:, which, t, HC * a:HC * a + HC],
                                          id_sb[0:PT, 0:PT])
                mm.then_inc(done, 1)

            def mlp(u, attn_u):
                pe.wait_ge(ln_dve[1], 3 * u + 3)
                transposes(1, t2_done)
                pe.wait_ge(h2_done, u + 1)
                for m in range(MC):
                    if attn_u is None:
                        if m >= 2:
                            pe.wait_ge(gelu_done, MC * u + m - 1)
                        else:
                            pe.wait_ge(x2_done, 2 * u + 2)
                    elif m < 2:
                        pe.wait_ge(v_evac, 4 * attn_u + 3 + m)
                    else:
                        pe.wait_ge(gelu_done, MC * u + m - 1)
                    for a in range(2):
                        mm = pe.matmul(ps[:, 6 + m % 2, 0:UT], w1_sb[:, a, 128 * m:128 * m + 128], h2T[:, a, :],
                                       start=(a == 0), stop=(a == 1))
                    mm.then_inc(h_full, 1)
                for a in range(2):
                    pe.wait_ge(gelu_done, MC * u + MC)
                    for m in range(MC):
                        pe.matmul(ps[0:HC, 4 + a, 0:UT], w2_sb[:, m, HC * a:HC * a + HC], g_sb[:, m, :],
                                  start=(m == 0), stop=False)
                    for t in range(NPAIR):
                        mm = pe.matmul(ps[0:HC, 4 + a, PT * t:PT * t + PT], x2[:, t, HC * a:HC * a + HC],
                                       id_sb[0:PT, 0:PT], start=False, stop=(t == NPAIR - 1))
                    mm.then_inc(m2_full, 1)

            def step(u, half, par, first, is_last):
                pe.wait_ge(ln_dve[0], 3 * u + 3)
                if not first:
                    pe.wait_ge(av_evac, u)
                transposes(0, t1_done)
                pe.wait_ge(xn_done, u + 1)
                for e in range(4):
                    if e >= 2:
                        pe.wait_ge(qk_evac, 4 * u + e - 1)
                    elif not first:
                        pe.wait_ge(x2_done, 2 * u - 1 + e)
                    for a in range(2):
                        mm = pe.matmul(ps[0:HC, 6 + e % 2, 0:UT], wqkv_sb[:, a, HC * e:HC * e + HC], xnT[:, a, :],
                                       start=(a == 0), stop=(a == 1))
                    mm.then_inc(qk_full, 1)
                for e in range(UW // 2):
                    if e < 2:
                        pe.wait_ge(qk_evac, 4 * u + 3 + e)
                    else:
                        pe.wait_ge(v_evac, 4 * u + e - 1)
                    for w in range(2):
                        for a in range(2):
                            tok = WT * (2 * e + w)
                            mm = pe.matmul(ps[0:WT, 6 + e % 2, C * w:C * w + C], xnT[:, a, tok:tok + WT],
                                           wqkv_sb[:, a, 2 * C:3 * C], start=(a == 0), stop=(a == 1))
                    mm.then_inc(v_full, 1)
                if not first:
                    pe.wait_ge(x1_done, 2 * u)
                for q in range(NPAIR):
                    if q >= 2:
                        pe.wait_ge(sub_done, NPAIR * u + q - 1)
                    for r in range(3):
                        for hh in range(2):
                            for w in range(2):
                                tok = PT * q + WT * w
                                mm = pe.matmul(score_rows(q, w, r, hh), qkT[32 * r:32 * r + 32, hh, tok:tok + WT],
                                               qkT[32 * r:32 * r + 32, 2 + hh, tok:tok + WT], start=True, stop=True)
                    mm.then_inc(s_full, 1)
                pe.wait_ge(sub_done, NPAIR * u + 4)
                if not first:
                    mlp(u - 1, u)
                for q in range(NPAIR + 1):
                    if q < NPAIR:
                        n = NPAIR * u + q
                        if q >= 1:
                            pe.wait_ge(pt_evac, n)
                        hold(pe, prob_done, n + 1, fence)
                        for hh in range(2):
                            for r in range(3):
                                mm = pe.transpose(ps[0:WT, 2 + hh, 128 * r:128 * r + 128], prob[:, q, r, hh, :],
                                                  id_sb[:, :])
                        mm.then_inc(pt_full, 1)
                    if q >= 1:
                        if q == 1 and not first:
                            pe.wait_ge(h2_done, u)
                        hold(pe, pt_evac, NPAIR * u + q, fence)
                        for hh in range(2):
                            for w in range(2):
                                for r in range(3):
                                    tok = PT * (q - 1) + WT * w
                                    mm = pe.matmul(ps[32 * r:32 * r + 32, hh, tok:tok + WT],
                                                   v_sb[:, 2 * (q - 1) + w, HC * hh + 32 * r:HC * hh + 32 * r + 32],
                                                   pT[:, (q - 1) % 2, hh, r, 64 * w:64 * w + WT], start=True, stop=True)
                mm.then_inc(av_full, 1)
                pe.wait_ge(av_evac, u + 1)
                for e in range(2):
                    if first:
                        pe.wait_ge(v_evac, 3 + e)
                    else:
                        pe.wait_ge(gelu_done, MC * u - 1 + e)
                    for t in range(2):
                        for a in range(2):
                            tok = PT * (2 * e + t)
                            mm = pe.matmul(ps[0:PT, 6 + e, C * t:C * t + C], oT[:, a, tok:tok + PT], wp_sb[:, a, :],
                                           start=(a == 0), stop=(a == 1))
                    mm.then_inc(pj_full, 1)

            def last(u, half, par):
                mlp(u - 1, None)

            units(pe, step, last)


def build_reorder(nc, scr_a, xs, n_img):
    with ExitStack() as ctx:
        sb = lambda name, shape, dt=F32: ctx.enter_context(nc.sbuf_tensor("b_" + name, shape, dt))
        sem = lambda name: ctx.enter_context(nc.semaphore(name))
        rolled = sb("rolled", [HC, 2, L])
        nat = sb("nat", [HC, 2, L])
        tra = sb("tra", [HC, 2, L])
        r_in = [sem("b_in0"), sem("b_in1")]
        nat_done, tra_done = sem("b_nat_done"), sem("b_tra_done")
        nat_out = [sem("b_nat_out0"), sem("b_nat_out1")]
        tra_out = [sem("b_tra_out0"), sem("b_tra_out1")]
        K = IMG - SHIFT
        pieces = [((0, K), (SHIFT, IMG)), ((K, IMG), (0, SHIFT))]
        fence = sem("reorde_fence")
        block = ctx.enter_context(nc.Block())

        @block.sync
        def _(sp):
            for a in range(2):
                sp.sem_inc(nat_out[a], 16)
                sp.sem_inc(tra_out[a], 16)

            def load(b, a):
                src = scr_a[bass.ds(b * UW, UW), HC * a:HC * a + HC, :].rearrange("u p t -> p u t")
                sp.dma_start(rolled[:, a].rearrange("p (u t) -> p u t", u=UW), src).then_inc(r_in[a], 16)

            def store(b, a, first):
                sp.wait_ge(nat_done, 2 * b + a + 1)
                sp.dma_start(xs[bass.ds(2 * b, 1), a].rearrange("u p t -> p (u t)"), nat[:, a]).then_inc(nat_out[a], 16)
                sp.wait_ge(tra_done, 2 * b + a + 1)
                sp.dma_start(xs[bass.ds(2 * b + 1, 1), a].rearrange("u p t -> p (u t)"), tra[:, a]).then_inc(tra_out[a], 16)

            for a in range(2):
                load(0, a)
            if n_img > 1:
                with sp.Fori(0, n_img - 1) as b:
                    for a in range(2):
                        store(b, a, False)
                        load(b + 1, a)
            for a in range(2):
                store(n_img - 1, a, False)
            for a in range(2):
                sp.wait_ge(nat_out[a], 16 * n_img + 16)
                sp.wait_ge(tra_out[a], 16 * n_img + 16)

        @block.scalar
        def _(act):
            with act.Fori(0, n_img) as b:
                for a in range(2):
                    act.wait_ge(r_in[a], 16 * b + 16)
                    act.wait_ge(nat_out[a], 16 * b + 16)
                    src = rolled[:, a].rearrange("p (h w) -> p h w", h=IMG)
                    dst = nat[:, a].rearrange("p (h w) -> p h w", h=IMG)
                    for (i0, i1), (h0, h1) in pieces:
                        for (j0, j1), (w0, w1) in pieces:
                            ins = nc.scalar.activation(dst[:, h0:h1, w0:w1], src[:, i0:i1, j0:j1], ACT.Copy)
                    ins.then_inc(nat_done, 1)

        @block.vector
        def _(dve):
            with dve.Fori(0, n_img) as b:
                for a in range(2):
                    dve.wait_ge(r_in[a], 16 * b + 16)
                    dve.wait_ge(tra_out[a], 16 * b + 16)
                    src = rolled[:, a].rearrange("p (h w) -> p h w", h=IMG)
                    dst = tra[:, a].rearrange("p (w h) -> p h w", h=IMG)
                    for (i0, i1), (h0, h1) in pieces:
                        for (j0, j1), (w0, w1) in pieces:
                            ins = nc.vector.tensor_copy(dst[:, h0:h1, w0:w1], src[:, i0:i1, j0:j1])
                    ins.then_inc(tra_done, 1)


def build_scan_weights(nc, io, wpk, apk):
    xpT, xpr, dtwT, dtb, a_log = io
    with ExitStack() as ctx:
        sb = lambda name, shape, dt=F32: ctx.enter_context(nc.sbuf_tensor("w_" + name, shape, dt))
        sem = lambda name: ctx.enter_context(nc.semaphore(name))
        ps = ctx.enter_context(nc.psum_tensor("w_psum", [HC, 8, 512], F32))
        xpT_sb = sb("xpT_sb", [HC, 4, 2, RANK + 2 * NS])
        xpr_sb = sb("xpr_sb", [RANK, 4, C])
        dtw_sb = sb("dtw_sb", [RANK, 4, C])
        al_sb = sb("al_sb", [128, 4, NG])
        pack = sb("pack", [HC, 4, WPK])
        w_in, w_mm, w_pk, w_exp, w_neg, w_out = (sem(n) for n in ("w_in", "w_mm", "w_pk", "w_exp", "w_neg", "w_out"))
        fence = sem("scanw_fence")
        block = ctx.enter_context(nc.Block())

        @block.sync
        def _(sp):
            sp.dma_start(xpT_sb[:], xpT).then_inc(w_in, 16)
            sp.dma_start(xpr_sb[:], xpr).then_inc(w_in, 16)
            sp.dma_start(dtw_sb[:], dtwT).then_inc(w_in, 16)
            sp.dma_start(al_sb[:], a_log).then_inc(w_in, 16)
            sp.dma_start(pack[:, :, WPK - 2:WPK], dtb).then_inc(w_in, 16)
            sp.wait_ge(w_in, 80)
            sp.wait_ge(w_pk, 1)
            sp.dma_start(wpk.rearrange("k p w -> p k w"), pack[:]).then_inc(w_out, 16)
            sp.wait_ge(w_neg, 1)
            sp.dma_start(apk.rearrange("k p g -> p k g"), al_sb[:]).then_inc(w_out, 16)
            sp.wait_ge(w_out, 32)

        @block.tensor
        def _(pe):
            pe.wait_ge(w_in, 80)
            for k in range(4):
                for a in range(2):
                    mm = pe.matmul(ps[:, 2 * k + a, 0:C], xpr_sb[:, k, HC * a:HC * a + HC], dtw_sb[:, k, :],
                                   start=True, stop=True)
            mm.then_inc(w_mm, 1)

        @block.vector
        def _(dve):
            dve.wait_ge(w_in, 80)
            for k in range(4):
                for m in range(2):
                    for a in range(2):
                        src = xpT_sb[:, k, a, RANK + NS * m:RANK + NS * m + NS].unsqueeze(2).to_broadcast([HC, NS, DG])
                        o = 2 * C + 256 * m + 128 * a
                        nc.vector.tensor_copy(pack[:, k, o:o + 128].rearrange("p (n d) -> p n d", d=DG), src)
            dve.wait_ge(w_mm, 1)
            for k in range(4):
                ins = nc.vector.tensor_copy(pack[:, k, 0:2 * C].rearrange("p (a d) -> p a d", a=2), ps[:, 2 * k:2 * k + 2, 0:C])
            ins.then_inc(w_pk, 1)
            dve.wait_ge(w_exp, 1)
            nc.vector.tensor_scalar(al_sb[:], al_sb[:], -1.0, None, ALU.mult).then_inc(w_neg, 1)

        @block.scalar
        def _(act):
            act.wait_ge(w_in, 80)
            nc.scalar.activation(al_sb[:], al_sb[:], ACT.Exp).then_inc(w_exp, 1)


def build_scan(nc, io, xs, wpk, apk, ysc, n_img):
    sel_h, red_h = io
    NSTEP = NG
    RA, RH, RP = 4, 4, 8
    NV = n_img * 2 * NCH * 2
    with ExitStack() as ctx:
        sb = lambda name, shape, dt=F32: ctx.enter_context(nc.sbuf_tensor("c_" + name, shape, dt))
        sem = lambda name: ctx.enter_context(nc.semaphore(name))
        ps = ctx.enter_context(nc.psum_tensor("c_psum", [128, 4096], F32))
        HT = CH // 2
        DH = [ps[:, 0:HT], ps[:, 512:512 + HT]]
        U = [ps[:, 1024:1024 + CH], ps[:, 2048:2048 + CH]]
        Y = ps[0:HC, 3072:3072 + CH]
        cuts = [(0, 512), (512, CH)]

        sel_f = sb("sel_f", [96, 4, 128])
        sel = sb("sel", [96, 4, 128], BF16)
        red = sb("red", [128, 4, 32])
        zero = sb("zero", [128, NG])
        one = sb("one", [HC, 1])
        x_u = sb("x_u", [HC, 2, 2, CH])
        w_u = sb("w_u", [HC, 2, WPK])
        a_u = sb("a_u", [128, 2, NG])
        init = sb("init", [128, 2, NG])
        lastc = sb("lastc", [128, 2, NG])
        bc = sb("bc", [128, 2, 2, CH])
        pk = sb("pk", [96, 2, 2, NQ, CH], BF16)
        e_t = sb("e_t", [HC, CH])
        rl_t = sb("rl_t", [HC, CH])
        l_t = sb("l_t", [HC, CH])
        w_t = sb("w_t", [HC, CH])
        du = sb("du", [HC, 2, CH])
        rem = sb("rem", [HC, 2, CH])
        parts = sb("parts", [HC, 2, 2, 3, CH], BF16)
        dA = sb("dA", [128, RA, CH])
        hs = sb("hs", [128, RH, CH])
        pr = sb("pr", [128, RP, CH])
        y_sb = sb("y_sb", [HC, 2, CH])

        const_in = sem("c_const")
        one_done = sem("c_one")
        sel_done = sem("c_sel")
        xw_in = [sem("c_xw_in0"), sem("c_xw_in1")]
        ai_in = [sem("c_ai_in0"), sem("c_ai_in1")]
        d_full, exp_done = sem("c_d_full"), sem("c_exp_done")
        u_full, mul_done, scan_done = sem("c_u_full"), sem("c_mul_done"), sem("c_scan_done")
        carry_done = sem("c_carry_done")
        prod_done = sem("c_prod_done")
        y_evac = sem("c_y_evac")
        y_out = [sem("c_y_out0"), sem("c_y_out1")]
        raw_full, raw_evac = sem("c_raw_full"), sem("c_raw_evac")
        act_sp = sem("c_act_sp")
        dve_sp = sem("c_dve_sp")
        dt_done = sem("c_dt_done")
        u_done = sem("c_u_done")
        hi_done, rem_done = sem("c_hi_done"), sem("c_rem_done")
        mid_done, lo_done = sem("c_mid_done"), sem("c_lo_done")
        pk_in = [[sem(f"c_pk_in{d}{a}") for a in range(2)] for d in range(2)]
        red_done = sem("c_red_done")
        N_PK = 16 * 9
        WI = 2 * NCH * 2
        ITEMS = [(k, t) for k in range(4) for t in range(2)]
        ITEM_AT = {0: 0, 1: 1, 6: 2, 7: 3, 10: 4, 12: 5, 14: 6, 16: 7}
        EXP_AT, LOG_AT = (2, 8), (3, 9)
        SP1_AT, SP2_AT = (4, 11), (5, 13)
        U_AT = (5, 13)
        HI_AT = {9: (0, 0), 11: (0, 1), 16: (1, 0), 18: (1, 1)}
        REM_AT = {10: (0, 0), 12: (0, 1), 17: (1, 0), 18: (1, 1)}
        MID_AT = {13: (0, 0), 15: (0, 1), 20: (1, 0), 21: (1, 1)}
        LO_AT = {13: (0, 0), 15: (0, 1), 20: (1, 0), 22: (1, 1)}
        RED_LAG = 8

        fence = sem("scan_fence")
        block = ctx.enter_context(nc.Block())

        def step_ids(s):
            hh, j, qq = s // 12, (s % 12) // 3, s % 3
            return hh, j, qq, 4 * (3 * hh + qq) + j

        @block.sync
        def _(sp):
            sp.dma_start(sel_f[:], sel_h).then_inc(const_in, 16)
            sp.dma_start(red[:], red_h).then_inc(const_in, 16)
            for a in range(2):
                sp.sem_inc(y_out[a], 16)

            def unit_of(w):
                o, c, d = w // (2 * NCH), w // 2 % NCH, w % 2
                return o, (c if d == 0 else NCH - 1 - c), d

            def load_xw(b, w):
                o, cc, d = unit_of(w)
                sp.dma_start(x_u[:, d], xs[bass.ds(2 * b + o, 1), :, :, CH * cc:CH * cc + CH].rearrange(
                    "u a p t -> p (u a) t")).then_inc(xw_in[d], 16)
                sp.dma_start(w_u[:, d], wpk[o + 2 * d]).then_inc(xw_in[d], 16)

            def load_ai(w):
                o, _, d = unit_of(w)
                sp.dma_start(a_u[:, d], apk[o + 2 * d]).then_inc(ai_in[d], 16)
                starts = w % (2 * NCH) < 2
                sp.dma_start(init[:, d], zero[:] if starts else lastc[:, d]).then_inc(ai_in[d], 16)

            def packs(v, w, a):
                d = w % 2
                sp.wait_ge(lo_done, 4 * v + 2 * a + 2)
                for k in range(3):
                    for q in range(3):
                        sp.dma_start(pk[32 * k:32 * k + 32, d, :, 3 * a + q, :],
                                     parts[32 * q:32 * q + 32, a, :, k, :]).then_inc(pk_in[d][a], 16)

            def store_y(b, v, w, a):
                o, cc, d = unit_of(w)
                sp.wait_ge(y_evac, 2 * v + a + 1)
                sp.dma_start(ysc[bass.ds(2 * b + o, 1), d, a, :, CH * cc:CH * cc + CH].rearrange("u p t -> (u p) t"),
                             y_sb[:, a]).then_inc(y_out[a], 16)

            def window(b, w, final):
                v = WI * b + w
                more1, more2 = not (final and w + 1 >= WI), not (final and w + 2 >= WI)
                if more2:
                    hold(sp, raw_evac, 8 * v + 8, fence)
                    hold(sp, u_done, 2 * v + 2, fence)
                    load_xw(b + (w + 2) // WI, (w + 2) % WI)
                if more1:
                    packs(v + 1, (w + 1) % WI, 0)
                store_y(b, v, w, 0)
                if more1:
                    packs(v + 1, (w + 1) % WI, 1)
                if more2:
                    hold(sp, exp_done, 2 * NSTEP * (v + 1), fence)
                    hold(sp, scan_done, NSTEP * (v + 1), fence)
                    hold(sp, carry_done, NSTEP * (v + 1), fence)
                    load_ai((w + 2) % WI)
                store_y(b, v, w, 1)

            sp.wait_ge(one_done, 1)
            for w in range(2):
                load_xw(0, w)
                load_ai(w)
            packs(0, 0, 0)
            packs(0, 0, 1)
            if n_img > 1:
                with sp.Fori(0, n_img - 1) as b:
                    for w in range(WI):
                        window(b, w, False)
            for w in range(WI):
                window(n_img - 1, w, True)
            for a in range(2):
                sp.wait_ge(y_out[a], 16 * NV + 16)

        def all_units(eng, unit):
            unit(0, 0, 0, True, False)
            with eng.Fori(0, NV // 2 - 1) as i:
                unit(2 * i + 1, i, 1, False, False)
                unit(2 * i + 2, i + 1, 0, False, False)
            unit(NV - 1, NV // 2 - 1, 1, False, True)

        @block.tensor
        def _(pe):
            pe.wait_ge(const_in, 32)
            pe.wait_ge(sel_done, 1)

            def prepare(v, h, d, i):
                k, t = ITEMS[i]
                if i == 0:
                    pe.wait_ge(xw_in[d], 32 * h + 32)
                for a in range(2):
                    o = C * a + HC * k if k < 2 else 2 * C + 256 * (k - 2) + 128 * a
                    n = HC if k < 2 else 128
                    mm = pe.matmul(DH[t][0:n, :], w_u[:, d, o:o + n], x_u[:, d, a, HT * t:HT * t + HT],
                                   start=(a == 0), stop=(a == 1))
                mm.then_inc(raw_full, 1)

            def reduce(v, m):
                if m % 4 == 0 and not (isinstance(v, int) and v == 0 and m == 0):
                    pe.wait_ge(y_evac, 2 * v + m // 4)
                pe.wait_ge(prod_done, NSTEP * v + 3 * m + 3)
                for n0, n1 in cuts:
                    for qq in range(3):
                        mm = pe.matmul(Y[32 * qq:32 * qq + 32, n0:n1], red[:, m % 4, :], pr[:, (3 * m + qq) % RP, n0:n1],
                                       start=(m % 4 == 0), stop=(m % 4 == 3))
                mm.then_inc(red_done, 1)

            for i in range(len(ITEMS)):
                if i >= 2:
                    pe.wait_ge(raw_evac, i - 1)
                prepare(0, 0, 0, i)

            def unit(v, h, d, first, last):
                for s in range(NSTEP):
                    hh, j, qq, _ = step_ids(s)
                    item = ITEM_AT.get(s - 1) if not last else None
                    for t in range(2):
                        if item is not None and ITEMS[item][1] == t:
                            pe.wait_ge(raw_evac, 8 * v + 8 + item + 1)
                        elif first and s == 0:
                            pe.wait_ge(raw_evac, 7 + t)
                        else:
                            pe.wait_ge(exp_done, 2 * (NSTEP * v + s) - 1 + t)
                        if s % 12 == 0 and t == 0:
                            pe.wait_ge(pk_in[d][hh], N_PK * h + N_PK)
                        pe.matmul(DH[t], sel[:, j, :], pk[:, d, 0, 3 * hh + qq, HT * t:HT * t + HT],
                                  start=True, stop=True).then_inc(d_full, 1)
                    if not (first and s < 2):
                        pe.wait_ge(scan_done, NSTEP * v + s - 1)
                    for n0, n1 in cuts:
                        mm = pe.matmul(U[s % 2][:, n0:n1], sel[:, j, :], pk[:, d, 1, 3 * hh + qq, n0:n1],
                                       start=True, stop=True)
                    mm.then_inc(u_full, 1)
                    if s in ITEM_AT and not last:
                        item = ITEM_AT[s]
                        pe.wait_ge(exp_done, 2 * (NSTEP * v + s) + 1 + ITEMS[item][1])
                        prepare(v + 1, h + d, 1 - d, item)
                    if not first and s + NSTEP - RED_LAG in (3 * 6, 3 * 7):
                        reduce(v - 1, (s + NSTEP - RED_LAG) // 3)
                    if s >= RED_LAG and (s - RED_LAG) % 3 == 0:
                        reduce(v, (s - RED_LAG) // 3)
                if last:
                    reduce(v, 6)
                    reduce(v, 7)

            all_units(pe, unit)

        @block.scalar
        def _(act):
            def item(v, h, d, i, start):
                k, t = ITEMS[i]
                now = slice(HT * t, HT * t + HT)
                act.wait_ge(raw_full, 8 * v + i + 1)
                if k < 2:
                    bias = w_u[:, d, WPK - 2 + k:WPK - 1 + k]
                    if t == 0 and not (start and k == 0):
                        act.wait_ge(dt_done, 2 * v + k)
                    nc.scalar.activation(e_t[:, now], DH[t][0:HC, :], ACT.Abs, bias=bias).then_inc(act_sp, 1)
                    nc.scalar.activation(rl_t[:, now], DH[t][0:HC, :], ACT.Relu, bias=bias).then_inc(raw_evac, 1)
                else:
                    if t == 0 and not start:
                        act.wait_ge(prod_done, NSTEP * (v - 1))
                    nc.scalar.activation(bc[:, d, k - 2, now], DH[t], ACT.Copy).then_inc(raw_evac, 1)

            def exponential(v, a):
                n = 10 * v + 5 * a
                act.wait_ge(act_sp, n + 2)
                nc.scalar.activation(e_t[:], e_t[:], ACT.Exp, scale=-1.0).then_inc(act_sp, 1)

            def logarithm(v, a):
                n = 10 * v + 5 * a
                act.wait_ge(act_sp, n + 3)
                nc.scalar.activation(w_t[:], e_t[:], ACT.Identity, bias=one[:, 0:1]).then_inc(act_sp, 1)
                act.wait_ge(act_sp, n + 4)
                nc.scalar.activation(l_t[:], w_t[:], ACT.Ln).then_inc(act_sp, 1)

            def high(v, h, d, a, m, start):
                if m == 0:
                    act.wait_ge(dt_done, 2 * v + a + 1)
                    if not start:
                        act.wait_ge(pk_in[1 - d][a], N_PK * h + N_PK * d)
                else:
                    act.wait_ge(u_done, 2 * v + a + 1)
                nc.scalar.activation(parts[:, a, m, 0, :], du[:, m, :], ACT.Copy).then_inc(hi_done, 1)

            def middle(v, a, m):
                act.wait_ge(rem_done, 4 * v + 2 * a + m + 1)
                nc.scalar.activation(parts[:, a, m, 1, :], rem[:, m, :], ACT.Copy).then_inc(mid_done, 1)

            def evacuate(v, a):
                act.wait_ge(red_done, 8 * v + 4 * a + 4)
                act.wait_ge(y_out[a], 16 * v + 16)
                nc.scalar.activation(y_sb[:, a], Y, ACT.Copy).then_inc(y_evac, 1)

            act.wait_ge(const_in, 32)
            nc.scalar.activation(sel[:], sel_f[:], ACT.Copy).then_inc(sel_done, 1)
            nc.scalar.preload_act_table_set(LN_EXP)
            act.wait_ge(one_done, 1)
            act.wait_ge(xw_in[0], 32)
            for a in range(2):
                item(0, 0, 0, 2 * a, True)
                item(0, 0, 0, 2 * a + 1, True)
                exponential(0, a)
                logarithm(0, a)
                for m in range(2):
                    high(0, 0, 0, a, m, True)
                for m in range(2):
                    middle(0, a, m)
            for i in range(4, 8):
                item(0, 0, 0, i, True)

            def unit(v, h, d, first, last):
                act.wait_ge(ai_in[d], 32 * h + 32)
                nh, nd = h + d, 1 - d
                for s in range(NSTEP):
                    col = step_ids(s)[3]
                    if not (first and s < RA):
                        act.wait_ge(scan_done, NSTEP * v + s + 1 - RA)
                    for t in range(2):
                        act.wait_ge(d_full, 2 * (NSTEP * v + s) + t + 1)
                        nc.scalar.activation(dA[:, s % RA, HT * t:HT * t + HT], DH[t], ACT.Exp,
                                             scale=a_u[:, d, col:col + 1]).then_inc(exp_done, 1)
                    if not last:
                        if s == 0:
                            act.wait_ge(xw_in[nd], 32 * nh + 32)
                        if s in ITEM_AT:
                            item(v + 1, nh, nd, ITEM_AT[s], first and ITEM_AT[s] >= 4)
                        if s in EXP_AT:
                            exponential(v + 1, EXP_AT.index(s))
                        if s in LOG_AT:
                            logarithm(v + 1, LOG_AT.index(s))
                        if s in HI_AT:
                            high(v + 1, nh, nd, *HI_AT[s], False)
                        if s in MID_AT:
                            middle(v + 1, *MID_AT[s])
                    if s == 7 and not first:
                        evacuate(v - 1, 1)
                    if s == 19:
                        evacuate(v, 0)
                if last:
                    evacuate(v, 1)

            all_units(act, unit)

        @block.vector
        def _(dve):
            nc.vector.memset(one[:], 1.0)
            nc.vector.memset(zero[:], 0.0).then_inc(one_done, 1)

            def softplus1(v, a):
                k = 2 * v + a
                dve.wait_ge(act_sp, 5 * k + 5)
                nc.vector.scalar_tensor_tensor(l_t[:], w_t[:], -1.0, l_t[:], ALU.add, ALU.min)
                nc.vector.scalar_tensor_tensor(w_t[:], w_t[:], -1.0, e_t[:], ALU.add, ALU.subtract).then_inc(dve_sp, 1)

            def softplus2(v, a, start):
                k = 2 * v + a
                dve.wait_ge(dve_sp, 2 * k + 1)
                nc.vector.tensor_tensor(w_t[:], l_t[:], w_t[:], ALU.subtract).then_inc(dve_sp, 1)
                dve.wait_ge(dve_sp, 2 * k + 2)
                dve.wait_ge(raw_evac, 8 * v + 2 * a + 2)
                if not (start and a == 0):
                    dve.wait_ge(hi_done, 2 * k)
                    dve.wait_ge(u_done, k)
                nc.vector.tensor_tensor(du[:, 0, :], w_t[:], rl_t[:], ALU.add).then_inc(dt_done, 1)

            def remainder(v, a, m, start):
                dve.wait_ge(hi_done, 4 * v + 2 * a + m + 1)
                if not (start and a == 0):
                    dve.wait_ge(lo_done, 4 * v + 2 * a)
                nc.vector.tensor_tensor(rem[:, m, :], du[:, m, :], parts[:, a, m, 0, :], ALU.subtract).then_inc(rem_done, 1)

            for a in range(2):
                softplus1(0, a)
                softplus2(0, a, True)
                remainder(0, a, 0, True)
                remainder(0, a, 1, True)

            def keep_state(v, d, s):
                col = CH - 1 if d == 0 else 0
                dve.wait_ge(scan_done, NSTEP * v + s + 1)
                nc.vector.tensor_copy(lastc[:, d, s:s + 1], hs[:, s % RH, col:col + 1]).then_inc(carry_done, 1)

            def unit(v, h, d, first, last):
                way = slice(None, None, 1 if d == 0 else -1)
                dve.wait_ge(raw_evac, 8 * v + 6)
                for s in range(NSTEP):
                    n = NSTEP * v + s
                    dve.wait_ge(u_full, n + 1)
                    nc.vector.tensor_tensor(U[s % 2], U[s % 2], bc[:, d, 0, :], ALU.mult).then_inc(mul_done, 1)
                    if s:
                        keep_state(v, d, s - 1)
                    elif not first:
                        keep_state(v - 1, 1 - d, NSTEP - 1)
                    if s == 0:
                        dve.wait_ge(ai_in[d], 32 * h + 32)
                    dve.wait_ge(exp_done, 2 * n + 2)
                    dve.wait_ge(mul_done, n + 1)
                    if not (first and s < RH):
                        dve.wait_ge(prod_done, n + 1 - RH)
                    nc.vector.tensor_tensor_scan(hs[:, s % RH, way], dA[:, s % RA, way], U[s % 2][:, way],
                                                 init[:, d, s:s + 1], ALU.mult, ALU.add).then_inc(scan_done, 1)
                    if not last:
                        if s in SP1_AT:
                            softplus1(v + 1, SP1_AT.index(s))
                        if s in REM_AT:
                            remainder(v + 1, *REM_AT[s], False)
                        if s in SP2_AT:
                            softplus2(v + 1, SP2_AT.index(s), False)

            all_units(dve, unit)

        @block.gpsimd
        def _(pool):
            def dt_x(v, h, d, a, start):
                pool.wait_ge(dt_done, 2 * v + a + 1)
                if a == 0:
                    pool.wait_ge(xw_in[d], 32 * h + 32)
                if not (start and a == 0):
                    pool.wait_ge(rem_done, 4 * v + 2 * a)
                nc.gpsimd.tensor_tensor(du[:, 1, :], du[:, 0, :], x_u[:, d, a, :], ALU.mult).then_inc(u_done, 1)

            def low(v, a, m):
                pool.wait_ge(mid_done, 4 * v + 2 * a + m + 1)
                nc.gpsimd.tensor_tensor(parts[:, a, m, 2, :], rem[:, m, :], parts[:, a, m, 1, :],
                                        ALU.subtract).then_inc(lo_done, 1)

            for a in range(2):
                dt_x(0, 0, 0, a, True)
                low(0, a, 0)
                low(0, a, 1)

            def unit(v, h, d, first, last):
                pool.wait_ge(raw_evac, 8 * v + 8)
                for s in range(NSTEP):
                    pool.wait_ge(scan_done, NSTEP * v + s + 1)
                    if not (first and s < RP):
                        pool.wait_ge(red_done, 8 * v + (s - RP) // 3 + 1)
                    nc.gpsimd.tensor_tensor(pr[:, s % RP, :], hs[:, s % RH, :], bc[:, d, 1, :], ALU.mult).then_inc(prod_done, 1)
                    if not last:
                        if s in U_AT:
                            dt_x(v + 1, h + d, 1 - d, U_AT.index(s), False)
                        if s in LO_AT:
                            low(v + 1, *LO_AT[s])

            all_units(pool, unit)


def build_output(nc, io, xs, ysc, out, n_img):
    ds_h, lnw, lnb, ident = io
    NGRP = NT // GT
    with ExitStack() as ctx:
        sb = lambda name, shape, dt=F32: ctx.enter_context(nc.sbuf_tensor("d_" + name, shape, dt))
        sem = lambda name: ctx.enter_context(nc.semaphore(name))
        ps = ctx.enter_context(nc.psum_tensor("d_psum", [TT, 8, 512], F32))
        yin = sb("yin", [HC, 2, 4, L])
        x_in = sb("x_in", [HC, 2, L])
        yf = sb("yf", [HC, 2, L])
        ds_sb = sb("ds_sb", [HC, 2, 4])
        dsum = sb("dsum", [HC, 2])
        w_sb = sb("w_sb", [TT, C])
        b_sb = sb("b_sb", [TT, C])
        id_sb = sb("id_sb", [HC, HC])
        eps_sb = sb("eps_sb", [TT, 1])
        stats = sb("stats", [TT, 2, GT, 6])
        mv = sb("mv", [TT, NGRP, GT, 2])
        lnv = sb("lnv", [TT, NGRP, GT])
        rstd = sb("rstd", [TT, NGRP, GT])
        ob = sb("ob", [TT, NGRP, GT * C])
        c_in = sem("d_c_in")
        y_in = [sem("d_y_in0"), sem("d_y_in1")]
        ready = sem("d_ready")
        row_done, col_done, add_done, yf_done = sem("d_row"), sem("d_col"), sem("d_add"), sem("d_yf")
        t_full, st_done, ag_done = sem("d_t_full"), sem("d_st"), sem("d_ag")
        ln_done, rs_done, nm_done = sem("d_ln"), sem("d_rs"), sem("d_nm")
        wm_done, o_done = sem("d_wm"), sem("d_o")
        o_out = [sem(f"d_o_out{g}") for g in range(NGRP)]
        tile_ps = lambda g, t: ps[:, 2 * (g % 4) + t // 2, C * (t % 2):C * (t % 2) + C]
        fence = sem("output_fence")
        block = ctx.enter_context(nc.Block())

        @block.sync
        def _(sp):
            for dst, src in ((ds_sb[:], ds_h), (id_sb[:], ident[0:HC, 0:HC]),
                             (w_sb[:], lnw.unsqueeze(0).to_broadcast([TT, C])),
                             (b_sb[:], lnb.unsqueeze(0).to_broadcast([TT, C]))):
                sp.dma_start(dst, src).then_inc(c_in, 16)

            def load(b, a):
                for o in range(2):
                    sp.dma_start(yin[:, a, 2 * o:2 * o + 2, :],
                                 ysc[bass.ds(2 * b + o, 1), :, a].rearrange("u d p t -> p (u d) t")).then_inc(y_in[a], 16)
                sp.dma_start(x_in[:, a], xs[bass.ds(2 * b, 1), a].rearrange("u p t -> p (u t)")).then_inc(y_in[a], 16)

            def stores(b):
                for g in range(NGRP):
                    sp.wait_ge(o_done, NGRP * b + g + 1)
                    dst = out[bass.ds(b, 1), TT * GT * g:TT * GT * (g + 1), :].rearrange("u (t p) c -> p (u t) c", p=TT)
                    sp.dma_start(dst, ob[:, g].rearrange("p (t c) -> p t c", t=GT)).then_inc(o_out[g], 16)

            load(0, 0)
            load(0, 1)
            if n_img > 1:
                with sp.Fori(0, n_img - 1) as b:
                    for a in range(2):
                        sp.wait_ge(yf_done, 2 * b + a + 1)
                        load(b + 1, a)
                    stores(b)
            stores(n_img - 1)
            for g in range(NGRP):
                sp.wait_ge(o_out[g], 16 * n_img + 16)

        def images(eng, body):
            body(0, True)
            if n_img > 1:
                with eng.Fori(1, n_img) as b:
                    body(b, False)

        @block.gpsimd
        def _(pool):
            pool.wait_ge(c_in, 64)
            for g in range(NGRP):
                pool.sem_inc(o_out[g], 16)

            def body(b, first):
                for a in range(2):
                    pool.wait_ge(y_in[a], 48 * b + 48)
                    nc.gpsimd.tensor_tensor(yin[:, a, 2], yin[:, a, 2], yin[:, a, 3], ALU.add).then_inc(col_done, 1)
                for g in range(NGRP):
                    n = NGRP * b + g
                    pool.wait_ge(nm_done, n + 1)
                    o = ob[:, g].rearrange("p (t c) -> p t c", t=GT)
                    nc.gpsimd.tensor_tensor(o, o, w_sb[:].unsqueeze(1).to_broadcast([TT, GT, C]), ALU.mult).then_inc(wm_done, 1)
                    pool.wait_ge(wm_done, n + 1)
                    nc.gpsimd.tensor_tensor(o, o, b_sb[:].unsqueeze(1).to_broadcast([TT, GT, C]), ALU.add).then_inc(o_done, 1)

            images(pool, body)

        @block.vector
        def _(dve):
            nc.vector.memset(eps_sb[:], LN_EPS).then_inc(ready, 1)
            dve.wait_ge(c_in, 64)
            nc.vector.tensor_reduce(dsum[:], ds_sb[:], AX_X, ALU.add).then_inc(ready, 1)
            dve.wait_ge(ready, 2)

            def body(b, first):
                for a in range(2):
                    n = 2 * b + a
                    dve.wait_ge(y_in[a], 48 * b + 48)
                    nc.vector.tensor_tensor(yin[:, a, 0], yin[:, a, 0], yin[:, a, 1], ALU.add).then_inc(row_done, 1)
                    dve.wait_ge(row_done, n + 1)
                    dve.wait_ge(col_done, n + 1)
                    sq = lambda ap, p: ap.rearrange(p, h=IMG)
                    nc.vector.tensor_tensor(sq(yin[:, a, 0], "p (h w) -> p h w"), sq(yin[:, a, 0], "p (h w) -> p h w"),
                                            sq(yin[:, a, 2], "p (w h) -> p h w"), ALU.add).then_inc(add_done, 1)
                    dve.wait_ge(add_done, n + 1)
                    if a == 0 and not first:
                        dve.wait_ge(t_full, NGRP * b)
                    nc.vector.scalar_tensor_tensor(yf[:, a], x_in[:, a], dsum[:, a:a + 1], yin[:, a, 0],
                                                   ALU.mult, ALU.add).then_inc(yf_done, 1)

                def stat(g):
                    n = NGRP * b + g
                    dve.wait_ge(t_full, n + 1)
                    for t in range(GT):
                        ins = nc.vector.bn_stats(stats[:, g % 2, t], tile_ps(g, t))
                    ins.then_inc(st_done, 1)
                    if g == 0 and not first:
                        dve.wait_ge(rs_done, NGRP * b)
                    hold(dve, st_done, n + 1, fence)
                    for t in range(GT):
                        ins = nc.vector.bn_aggr(mv[:, g, t], stats[:, g % 2, t])
                    ins.then_inc(ag_done, 1)

                def normalise(g):
                    n = NGRP * b + g
                    dve.wait_ge(rs_done, n + 1)
                    dve.wait_ge(o_out[g], 16 * b + 16)
                    for t in range(GT):
                        ins = nc.vector.tensor_scalar(ob[:, g, C * t:C * t + C], tile_ps(g, t), mv[:, g, t, 0:1],
                                                      rstd[:, g, t:t + 1], ALU.subtract, ALU.mult)
                    ins.then_inc(nm_done, 1)

                for g in range(NGRP):
                    stat(g)
                    if g:
                        normalise(g - 1)
                normalise(NGRP - 1)

            images(dve, body)

        @block.scalar
        def _(act):
            act.wait_ge(ready, 1)
            nc.scalar.preload_act_table_set(LN_EXP)

            def body(b, first):
                for g in range(NGRP):
                    n = NGRP * b + g
                    act.wait_ge(ag_done, n + 1)
                    nc.scalar.activation(lnv[:, g], mv[:, g, :, 1], ACT.Ln, bias=eps_sb[:, 0:1]).then_inc(ln_done, 1)
                    act.wait_ge(ln_done, n + 1)
                    if g == 0 and not first:
                        act.wait_ge(nm_done, NGRP * b)
                    nc.scalar.activation(rstd[:, g], lnv[:, g], ACT.Exp, scale=-0.5).then_inc(rs_done, 1)

            images(act, body)

        @block.tensor
        def _(pe):
            pe.wait_ge(c_in, 64)

            def body(b, first):
                pe.wait_ge(yf_done, 2 * b + 2)
                for g in range(NGRP):
                    n = NGRP * b + g
                    if g >= 4:
                        pe.wait_ge(nm_done, n - 3)
                    elif not first and g < 4:
                        pe.wait_ge(nm_done, NGRP * b)
                    for t in range(GT):
                        for a in range(2):
                            tok = TT * (GT * g + t)
                            mm = pe.transpose(tile_ps(g, t)[:, HC * a:HC * a + HC], yf[:, a, tok:tok + TT], id_sb[:])
                    mm.then_inc(t_full, 1)

            images(pe, body)


def build(nc, ins, out, n_img):
    n_units = n_img * UW
    scr_a = nc.dram_tensor("scr_layer0", (n_units, C, UT), F32, kind="Internal").ap()
    xs = nc.dram_tensor("scr_x", (2 * n_img, 2, HC, L), F32, kind="Internal").ap()
    ysc = nc.dram_tensor("scr_y", (2 * n_img, 2, 2, HC, L), F32, kind="Internal").ap()
    wpk = nc.dram_tensor("scr_w", (4, HC, WPK), F32, kind="Internal").ap()
    apk = nc.dram_tensor("scr_a_neg", (4, 128, NG), F32, kind="Internal").ap()
    i = ins
    build_layer0(nc, (i["x_win"], i["qkv_w"], i["proj_w"], i["w1"], i["w2"], i["cols0"], i["b1c"], i["proj_b"],
                      i["ident"]), scr_a, n_units)
    build_reorder(nc, scr_a, xs, n_img)
    build_scan_weights(nc, (i["xpT"], i["xpr"], i["dtwT"], i["dtb"], i["a_log"]), wpk, apk)
    build_scan(nc, (i["sel"], i["red"]), xs, wpk, apk, ysc, n_img)
    build_output(nc, (i["ds"], i["ln_w"], i["ln_b"], i["ident"]), xs, ysc, out, n_img)


def lay_out(inputs):
    import numpy as np
    g = lambda n: np.asarray(inputs[n])
    x = g("x")
    n_img = x.shape[0]
    xw = np.roll(x, (-SHIFT, -SHIFT), axis=(1, 2)).reshape(n_img, UW, WS, UW, WS, C).transpose(0, 1, 3, 2, 4, 5)
    halves = lambda v: v.reshape(-1, HC).T
    cols0 = np.concatenate([halves(g("L0_conv_" + n)) for n in
                            ("ln1_w", "ln1_b", "qkv_b", "ln2_w", "ln2_b", "mlp_b2")], axis=1)
    xp, dtw, dtb = g("L1_conv_x_proj_weight"), g("L1_conv_dt_projs_weight"), g("L1_conv_dt_projs_bias")
    eye = np.eye(128, dtype=np.float32)
    sel = np.zeros((3, 4, DG, 4, NS, DG), np.float32)
    red = np.zeros((NS, DG, 4, 4, DG), np.float32)
    for j in range(4):
        for d in range(DG):
            sel[:, j, d, j, :, d] = 1
            red[:, d, j, j, d] = 1
    return {
        "x_win": xw.reshape(-1, C),
        "qkv_w": g("L0_conv_qkv_w"), "proj_w": g("L0_conv_proj_w"), "w1": g("L0_conv_mlp_w1"), "w2": g("L0_conv_mlp_w2"),
        "cols0": cols0, "b1c": g("L0_conv_mlp_b1").reshape(MC, 128).T, "proj_b": g("L0_conv_proj_b"), "ident": eye,
        "xpT": xp.reshape(4, RANK + 2 * NS, 2, HC).transpose(3, 0, 2, 1),
        "xpr": xp[:, :RANK].transpose(1, 0, 2), "dtwT": dtw.transpose(2, 0, 1),
        "dtb": dtb.reshape(4, 2, HC).transpose(2, 0, 1),
        "a_log": g("L1_conv_A_logs").reshape(4, NG, DG, NS).transpose(3, 2, 0, 1).reshape(128, 4, NG),
        "sel": sel.reshape(96, 4, 128), "red": red.reshape(128, 4, 32),
        "ds": g("L1_conv_Ds").reshape(4, 2, HC).transpose(2, 1, 0),
        "ln_w": g("L1_conv_ln_weight"), "ln_b": g("L1_conv_ln_bias"),
    }


def program(nc, arrays, n_img):
    import numpy as np
    ins = {n: nc.dram_tensor(f"in_{n}", a.shape, mybir.dt.from_np(a.dtype), kind="ExternalInput").ap()
           for n, a in arrays.items()}
    out = nc.dram_tensor("out", (n_img, L, C), F32, kind="ExternalOutput").ap()
    build(nc, ins, out, n_img)


def kernel(**inputs):
    import numpy as np
    from concourse import bacc
    from concourse.bass_utils import run_bass_kernel_spmd
    arrays = {n: np.ascontiguousarray(a) for n, a in lay_out(inputs).items()}
    n_img = np.asarray(inputs["x"]).shape[0]
    nc = bacc.Bacc("TRN2", target_bir_lowering=False, num_devices=1)
    program(nc, arrays, n_img)
    r = run_bass_kernel_spmd(nc, [{f"in_{n}": a for n, a in arrays.items()}], core_ids=[0])
    return r.results[0]["out"].reshape(n_img, IMG, IMG, C)
```

```python
from contextlib import ExitStack

import concourse.bass as bass
from concourse import mybir

ALU = mybir.AluOpType
ACT = mybir.ActivationFunctionType
AX_X = mybir.AxisListType.X
F32 = mybir.dt.float32
BF16 = mybir.dt.bfloat16

C = 192
HC = C // 2
IMG = 56
L = IMG * IMG
WS, SHIFT, NH = 7, 3, 6
HD = C // NH
WT = WS * WS
UW = IMG // WS
UT = UW * WT
PT = 2 * WT
WP = 64
NPAIR = UW // 2
HID = 4 * C
MC = HID // 128
SCALE = HD ** -0.5
LN_EPS = 1e-5

NS = 16
RANK = 12
LN_EXP = "natural_log_exp_and_others"
CH = 784
NCH = L // CH
DG = 8
NG = C // DG
NQ = C // 32
WPK = 2 * (C + 256) + 2

TT = 2 * IMG
NT = L // TT
GT = 4


def hold(eng, sem, value, fence):
    eng.wait_ge(sem, value)
    eng.sem_inc(fence, 1)


def build_layer0(nc, io, scr_a, n_units):
    x_win, w_qkv, w_proj, w1, w2, cols0, b1c, pb, ident = io
    with ExitStack() as ctx:
        sb = lambda name, shape, dt=F32: ctx.enter_context(nc.sbuf_tensor("a_" + name, shape, dt))
        sem = lambda name: ctx.enter_context(nc.semaphore(name))
        ps = ctx.enter_context(nc.psum_tensor("a_psum", [128, 8, 512], F32))

        wqkv_sb = sb("wqkv_sb", [HC, 2, 3 * C])
        wp_sb = sb("wp_sb", [HC, 2, C])
        w1_sb = sb("w1_sb", [HC, 2, HID])
        w2_sb = sb("w2_sb", [128, MC, C])
        cols = sb("cols", [HC, 16])
        b1_sb = sb("b1_sb", [128, MC])
        pb_sb = sb("pb_sb", [PT, C])
        id_sb = sb("id_sb", [128, 128])
        eps_sb = sb("eps_sb", [128, 1])
        x_sb = sb("x_sb", [PT, 2, NPAIR, C])
        xpb = sb("xpb", [PT, NPAIR, C])
        stats = sb("stats", [PT, 2, NPAIR, 6])
        mv = sb("mv", [PT, 2, NPAIR, 2])
        lnv = sb("lnv", [PT, 2, NPAIR])
        rstd = sb("rstd", [PT, 2, NPAIR])
        xhat = sb("xhat", [PT, 2, NPAIR, C])
        xnT = sb("xnT", [HC, 2, UW, WP])
        qkT = sb("qkT", [HC, 4, UT])
        v_sb = sb("v_sb", [WT, UW, C])
        prob = sb("prob", [128, NPAIR, 3, 2, WT])
        mx = sb("mx", [128, NPAIR, 3, 2])
        sm = sb("sm", [128, NPAIR, 3, 2])
        rs = sb("rs", [128, NPAIR, 3, 2])
        pT = sb("pT", [WT, 2, 2, 3, 128])
        oT = sb("oT", [HC, 2, UT])
        x2 = sb("x2", [PT, NPAIR, C])
        h2T = sb("h2T", [HC, 2, UT])
        g_sb = sb("g_sb", [128, MC, UT])
        x1T = sb("x1T", [HC, 2, 2, UT])

        scores = lambda q: ps[:, 3 * (q % 2):3 * (q % 2) + 3, 0:2 * WT].rearrange("p r (a k) -> p r a k", a=2)
        score_rows = lambda q, w, r, hh: ps[WP * w:WP * w + WT, 3 * (q % 2) + r, WT * hh:WT * hh + WT]
        LN1W, LN1B, QKB, VB, LN2W, LN2B, B2 = 0, 2, 4, 8, 10, 12, 14

        w_in = sem("a_w_in")
        x_in = [sem("a_x_in0"), sem("a_x_in1")]
        x1_out = [sem("a_x1_out0"), sem("a_x1_out1")]
        ready = sem("a_ready")
        xpb_done = sem("a_xpb_done")
        ln_dve = [sem("a_ln1_dve"), sem("a_ln2_dve")]
        ln_act = [sem("a_ln1_act"), sem("a_ln2_act")]
        t1_done, t2_done = sem("a_t1_done"), sem("a_t2_done")
        xn_done, h2_done = sem("a_xn_done"), sem("a_h2_done")
        qk_full, qk_evac = sem("a_qk_full"), sem("a_qk_evac")
        v_full, v_evac = sem("a_v_full"), sem("a_v_evac")
        s_full = sem("a_s_full")
        max_done, sub_done, exp_done = sem("a_max"), sem("a_sub"), sem("a_exp")
        sum_done, rec_done, prob_done = sem("a_sum"), sem("a_rec"), sem("a_prob")
        pt_full, pt_evac = sem("a_pt_full"), sem("a_pt_evac")
        av_full, av_evac = sem("a_av_full"), sem("a_av_evac")
        pj_full, x2_done = sem("a_pj_full"), sem("a_x2_done")
        h_full, gelu_done = sem("a_h_full"), sem("a_gelu")
        m2_full, x1_done = sem("a_m2_full"), sem("a_x1_done")

        def units(eng, step, last):
            step(0, 0, 0, True, n_units == 1)
            with eng.Fori(0, n_units // 2 - 1) as i:
                step(2 * i + 1, i, 1, False, False)
                step(2 * i + 2, i + 1, 0, False, False)
            step(n_units - 1, n_units // 2 - 1, 1, False, True)
            last(n_units, n_units // 2, 0)

        fence = sem("layer0_fence")
        block = ctx.enter_context(nc.Block())

        @block.sync
        def _(sp):
            for dst, src in ((wqkv_sb[:], w_qkv.rearrange("(a p) n -> p a n", a=2)),
                             (wp_sb[:], w_proj.rearrange("(a p) n -> p a n", a=2)),
                             (w1_sb[:], w1.rearrange("(a p) n -> p a n", a=2)),
                             (w2_sb[:], w2.rearrange("(a p) n -> p a n", a=MC)),
                             (cols[:], cols0), (b1_sb[:], b1c), (id_sb[:], ident),
                             (pb_sb[:], pb.unsqueeze(0).to_broadcast([PT, C]))):
                sp.dma_start(dst, src).then_inc(w_in, 16)

            def load(u, par):
                src = x_win[bass.ds(u * UT, UT), :].rearrange("(t p) c -> p t c", p=PT)
                sp.dma_start(x_sb[:, par], src).then_inc(x_in[par], 16)

            def store(u, par):
                dst = scr_a[bass.ds(u, 1)].rearrange("u (a p) t -> p (u a) t", a=2)
                sp.dma_start(dst, x1T[:, par]).then_inc(x1_out[par], 16)

            sp.sem_inc(x1_out[0], 16)
            sp.sem_inc(x1_out[1], 16)
            load(0, 0)

            def step(u, half, par, first, is_last):
                if not is_last:
                    if not first:
                        sp.wait_ge(ln_dve[0], 3 * u)
                        sp.wait_ge(xpb_done, u)
                    load(u + 1, 1 - par)
                if not first:
                    sp.wait_ge(x1_done, 2 * u)
                    store(u - 1, 1 - par)

            def last(u, half, par):
                sp.wait_ge(x1_done, 2 * u)
                store(u - 1, 1 - par)
                sp.wait_ge(x1_out[0], 16 * half + 16)
                sp.wait_ge(x1_out[1], 16 * half + 16)

            units(sp, step, last)

        @block.gpsimd
        def _(pool):
            pool.wait_ge(w_in, 16 * 8)

            def step(u, half, par, first, is_last):
                pool.wait_ge(x_in[par], 16 * half + 16)
                if not first:
                    pool.wait_ge(x2_done, 2 * u)
                nc.gpsimd.tensor_tensor(xpb[:], x_sb[:, par], pb_sb[:].unsqueeze(1).to_broadcast([PT, NPAIR, C]),
                                        ALU.add).then_inc(xpb_done, 1)

            units(pool, step, lambda *a: None)

        @block.vector
        def _(dve):
            nc.vector.memset(ps[:, 0:6, :], 0.0)
            nc.vector.memset(xnT[:], 0.0)
            nc.vector.memset(eps_sb[:], LN_EPS).then_inc(ready, 1)

            def norm(which, u, src):
                for t in range(NPAIR):
                    ins = nc.vector.bn_stats(stats[:, which, t, :], src[:, t, :])
                ins.then_inc(ln_dve[which], 1)
                hold(dve, ln_dve[which], 3 * u + 1, fence)
                for t in range(NPAIR):
                    ins = nc.vector.bn_aggr(mv[:, which, t, :], stats[:, which, t, :])
                ins.then_inc(ln_dve[which], 1)
                dve.wait_ge(ln_act[which], 2 * u + 2)
                dve.wait_ge(ln_dve[which], 3 * u + 2)
                for t in range(NPAIR):
                    ins = nc.vector.tensor_scalar(xhat[:, which, t, :], src[:, t, :], mv[:, which, t, 0:1],
                                                  rstd[:, which, t:t + 1], ALU.subtract, ALU.mult)
                ins.then_inc(ln_dve[which], 1)

            def norm1(u, half, par):
                dve.wait_ge(x_in[par], 16 * half + 16)
                if not (isinstance(u, int) and u == 0):
                    dve.wait_ge(t1_done, u)
                norm(0, u, x_sb[:, par])

            def front(u, q):
                n = NPAIR * u + q
                dve.wait_ge(s_full, n + 1)
                nc.vector.tensor_reduce(mx[:, q], scores(q), AX_X, ALU.max).then_inc(max_done, 1)
                dve.wait_ge(max_done, n + 1)
                nc.vector.tensor_tensor(prob[:, q], scores(q), mx[:, q].unsqueeze(3).to_broadcast([128, 3, 2, WT]),
                                        ALU.subtract).then_inc(sub_done, 1)

            def back(u, q):
                n = NPAIR * u + q
                dve.wait_ge(exp_done, n + 1)
                nc.vector.tensor_reduce(sm[:, q], prob[:, q], AX_X, ALU.add).then_inc(sum_done, 1)
                dve.wait_ge(sum_done, n + 1)
                nc.vector.reciprocal(rs[:, q], sm[:, q]).then_inc(rec_done, 1)
                dve.wait_ge(rec_done, n + 1)
                nc.vector.tensor_tensor(prob[:, q], prob[:, q], rs[:, q].unsqueeze(3).to_broadcast([128, 3, 2, WT]),
                                        ALU.mult).then_inc(prob_done, 1)

            norm1(0, 0, 0)

            def step(u, half, par, first, is_last):
                if not first:
                    dve.wait_ge(t2_done, u)
                    dve.wait_ge(x2_done, 2 * u)
                    norm(1, u - 1, x2[:])
                if not is_last:
                    norm1(u + 1, half + par, 1 - par)
                for e in range(UW // 2):
                    dve.wait_ge(v_full, UW // 2 * u + e + 1)
                    if e == 0 and not first:
                        dve.wait_ge(av_full, u)
                    for w in range(2):
                        ins = nc.vector.tensor_copy(v_sb[:, 2 * e + w, :], ps[WP * w:WP * w + WT, 6 + e % 2, 0:C])
                    ins.then_inc(v_evac, 1)
                if not first:
                    dve.wait_ge(pt_full, NPAIR * u)
                front(u, 0)
                for q in range(1, NPAIR):
                    front(u, q)
                    back(u, q - 1)
                back(u, NPAIR - 1)
                for q in range(NPAIR):
                    n = NPAIR * u + q
                    dve.wait_ge(pt_full, n + 1)
                    nc.vector.tensor_copy(pT[:, q % 2, 0], ps[0:WT, 2, 0:384].rearrange("p (r k) -> p r k", r=3))
                    nc.vector.tensor_copy(pT[:, q % 2, 1], ps[0:WT, 3, 0:384].rearrange("p (r k) -> p r k", r=3)
                                          ).then_inc(pt_evac, 1)
                if not first:
                    dve.wait_ge(m2_full, 2 * u)
                dve.wait_ge(xpb_done, u + 1)
                for e in range(2):
                    dve.wait_ge(pj_full, 2 * u + e + 1)
                    nc.vector.tensor_tensor(x2[:, 2 * e:2 * e + 2, :], xpb[:, 2 * e:2 * e + 2, :],
                                            ps[0:PT, 6 + e, 0:2 * C].rearrange("p (t c) -> p t c", t=2),
                                            ALU.add).then_inc(x2_done, 1)

            def last(u, half, par):
                dve.wait_ge(t2_done, u)
                dve.wait_ge(x2_done, 2 * u)
                norm(1, u - 1, x2[:])

            units(dve, step, last)

        @block.scalar
        def _(act):
            act.wait_ge(w_in, 16 * 8)
            act.wait_ge(ready, 1)

            def rstd_of(which, u):
                act.wait_ge(ln_dve[which], 3 * u + 2)
                nc.scalar.activation(lnv[:, which, :], mv[:, which, :, 1], ACT.Ln,
                                     bias=eps_sb[0:PT, :]).then_inc(ln_act[which], 1)
                act.wait_ge(ln_act[which], 2 * u + 1)
                nc.scalar.activation(rstd[:, which, :], lnv[:, which, :], ACT.Exp,
                                     scale=-0.5).then_inc(ln_act[which], 1)

            def affine(dst, bank, wcol, bcol, done):
                for a in range(2):
                    ins = nc.scalar.activation(dst(a), ps[0:HC, bank + a, 0:UT].rearrange("p (w k) -> p w k", w=UW), ACT.Identity,
                                               bias=cols[:, bcol + a:bcol + a + 1], scale=cols[:, wcol + a:wcol + a + 1])
                ins.then_inc(done, 1)

            def norm1_affine(u, first):
                act.wait_ge(t1_done, u + 1)
                if not first:
                    act.wait_ge(v_full, UW // 2 * u)
                affine(lambda a: xnT[:, a, :, 0:WT], 2, LN1W, LN1B, xn_done)

            def norm2_affine(u):
                act.wait_ge(t2_done, u + 2)
                affine(lambda a: h2T[:, a, :].rearrange("p (w k) -> p w k", w=UW), 0, LN2W, LN2B, h2_done)

            def gelus(u):
                for m in range(MC):
                    act.wait_ge(h_full, MC * u + m + 1)
                    nc.scalar.activation(g_sb[:, m, :], ps[:, 6 + m % 2, 0:UT], ACT.Gelu,
                                         bias=b1_sb[:, m:m + 1]).then_inc(gelu_done, 1)
                nc.scalar.preload_act_table_set(LN_EXP)

            def result(u, half, par):
                for a in range(2):
                    act.wait_ge(m2_full, 2 * u + a + 1)
                    if a == 0:
                        act.wait_ge(x1_out[par], 16 * half + 16)
                    nc.scalar.activation(x1T[:, par, a, :].rearrange("p (i w j) -> p w i j", i=WS, w=UW),
                                         ps[0:HC, 6 + a, 0:UT].rearrange("p (w i j) -> p w i j", w=UW, i=WS),
                                         ACT.Identity, bias=cols[:, B2 + a:B2 + a + 1]).then_inc(x1_done, 1)

            nc.scalar.preload_act_table_set(LN_EXP)
            rstd_of(0, 0)
            norm1_affine(0, True)

            def step(u, half, par, first, is_last):
                if not first:
                    rstd_of(1, u - 1)
                for e in range(4):
                    act.wait_ge(qk_full, 4 * u + e + 1)
                    if e == 0 and not first:
                        act.wait_ge(s_full, NPAIR * u)
                    nc.scalar.activation(qkT[:, e, :], ps[0:HC, 6 + e % 2, 0:UT], ACT.Identity,
                                         bias=cols[:, QKB + e:QKB + e + 1]).then_inc(qk_evac, 1)
                    if e == 2 and not is_last:
                        rstd_of(0, u + 1)
                if not first:
                    norm2_affine(u - 1)
                    gelus(u - 1)
                for q in range(NPAIR):
                    act.wait_ge(sub_done, NPAIR * u + q + 1)
                    nc.scalar.activation(prob[:, q], prob[:, q], ACT.Exp, scale=SCALE).then_inc(exp_done, 1)
                if not first:
                    result(u - 1, half - (1 - par), 1 - par)
                act.wait_ge(av_full, u + 1)
                if not first:
                    act.wait_ge(pj_full, 2 * u)
                for a in range(2):
                    ins = nc.scalar.activation(oT[:, a, :], ps[0:HC, a, 0:UT], ACT.Identity,
                                               bias=cols[:, VB + a:VB + a + 1])
                ins.then_inc(av_evac, 1)
                if not is_last:
                    norm1_affine(u + 1, False)

            def last(u, half, par):
                rstd_of(1, u - 1)
                norm2_affine(u - 1)
                gelus(u - 1)
                result(u - 1, half - 1, 1)

            units(act, step, last)

        @block.tensor
        def _(pe):
            pe.wait_ge(w_in, 16 * 8)
            pe.wait_ge(ready, 1)
            pe.sem_inc(t2_done, 1)

            def transposes(which, bank, done):
                for t in range(NPAIR):
                    for a in range(2):
                        mm = pe.transpose(ps[0:HC, bank + a, PT * t:PT * t + PT], xhat[:, which, t, HC * a:HC * a + HC],
                                          id_sb[0:PT, 0:PT])
                mm.then_inc(done, 1)

            def norm1_transposes(u):
                pe.wait_ge(ln_dve[0], 3 * u + 3)
                transposes(0, 2, t1_done)

            def norm2_transposes(u):
                pe.wait_ge(ln_dve[1], 3 * u + 3)
                transposes(1, 0, t2_done)

            def mlp_in(u, attn_u):
                pe.wait_ge(h2_done, u + 1)
                for m in range(MC):
                    if m >= 2:
                        pe.wait_ge(gelu_done, MC * u + m - 1)
                    elif attn_u is None:
                        pe.wait_ge(x2_done, 2 * u + 2)
                    else:
                        pe.wait_ge(v_evac, 4 * attn_u + 3 + m)
                    for a in range(2):
                        mm = pe.matmul(ps[:, 6 + m % 2, 0:UT], w1_sb[:, a, 128 * m:128 * m + 128], h2T[:, a, :],
                                       start=(a == 0), stop=(a == 1))
                    mm.then_inc(h_full, 1)

            def mlp_out(u, a, part):
                if a == 0 and part == 0:
                    pe.wait_ge(gelu_done, MC * u + MC)
                for m in (2 * part, 2 * part + 1):
                    pe.matmul(ps[0:HC, 6 + a, 0:UT], w2_sb[:, m, HC * a:HC * a + HC], g_sb[:, m, :],
                              start=(m == 0), stop=False)
                if part == 2:
                    for t in range(NPAIR):
                        mm = pe.matmul(ps[0:HC, 6 + a, PT * t:PT * t + PT], x2[:, t, HC * a:HC * a + HC],
                                       id_sb[0:PT, 0:PT], start=False, stop=(t == NPAIR - 1))
                    mm.then_inc(m2_full, 1)

            def pair_scores(u, q):
                if q >= 2:
                    pe.wait_ge(sub_done, NPAIR * u + q - 1)
                for r in range(3):
                    for hh in range(2):
                        for w in range(2):
                            tok = PT * q + WT * w
                            mm = pe.matmul(score_rows(q, w, r, hh), qkT[32 * r:32 * r + 32, hh, tok:tok + WT],
                                           qkT[32 * r:32 * r + 32, 2 + hh, tok:tok + WT], start=True, stop=True)
                mm.then_inc(s_full, 1)

            norm1_transposes(0)

            def step(u, half, par, first, is_last):
                pe.wait_ge(xn_done, u + 1)
                for e in range(4):
                    if e >= 2:
                        pe.wait_ge(qk_evac, 4 * u + e - 1)
                    elif not first:
                        pe.wait_ge(x2_done, 2 * u - 1 + e)
                    for a in range(2):
                        mm = pe.matmul(ps[0:HC, 6 + e % 2, 0:UT], wqkv_sb[:, a, HC * e:HC * e + HC], xnT[:, a, :, 0:WT],
                                       start=(a == 0), stop=(a == 1))
                    mm.then_inc(qk_full, 1)
                if not first:
                    norm2_transposes(u - 1)
                for e in range(UW // 2):
                    if e < 2:
                        pe.wait_ge(qk_evac, 4 * u + 3 + e)
                    else:
                        pe.wait_ge(v_evac, 4 * u + e - 1)
                    for a in range(2):
                        mm = pe.matmul(ps[:, 6 + e % 2, 0:C], xnT[:, a, 2 * e:2 * e + 2, :].rearrange("p w k -> p (w k)"),
                                       wqkv_sb[:, a, 2 * C:3 * C], start=(a == 0), stop=(a == 1))
                    mm.then_inc(v_full, 1)
                if not first:
                    mlp_in(u - 1, u)
                pair_scores(u, 0)
                pair_scores(u, 1)
                for q in (2, 3):
                    if not first:
                        mlp_out(u - 1, 0, q - 2)
                    pair_scores(u, q)
                if not first:
                    mlp_out(u - 1, 0, 2)
                for q in range(NPAIR + 1):
                    if q < NPAIR:
                        n = NPAIR * u + q
                        if q >= 1:
                            pe.wait_ge(pt_evac, n)
                        else:
                            pe.wait_ge(sub_done, NPAIR * u + NPAIR)
                        hold(pe, prob_done, n + 1, fence)
                        for hh in range(2):
                            for r in range(3):
                                mm = pe.transpose(ps[0:WT, 2 + hh, 128 * r:128 * r + 128], prob[:, q, r, hh, :],
                                                  id_sb[:, :])
                        mm.then_inc(pt_full, 1)
                        if q < 3 and not first:
                            mlp_out(u - 1, 1, q)
                    if q >= 1:
                        hold(pe, pt_evac, NPAIR * u + q, fence)
                        for hh in range(2):
                            for w in range(2):
                                for r in range(3):
                                    tok = PT * (q - 1) + WT * w
                                    mm = pe.matmul(ps[32 * r:32 * r + 32, hh, tok:tok + WT],
                                                   v_sb[:, 2 * (q - 1) + w, HC * hh + 32 * r:HC * hh + 32 * r + 32],
                                                   pT[:, (q - 1) % 2, hh, r, WP * w:WP * w + WT], start=True, stop=True)
                mm.then_inc(av_full, 1)
                if not is_last:
                    norm1_transposes(u + 1)
                pe.wait_ge(av_evac, u + 1)
                for e in range(2):
                    if first:
                        pe.wait_ge(v_evac, 3 + e)
                    else:
                        pe.wait_ge(x1_done, 2 * u - 1 + e)
                    for t in range(2):
                        for a in range(2):
                            tok = PT * (2 * e + t)
                            mm = pe.matmul(ps[0:PT, 6 + e, C * t:C * t + C], oT[:, a, tok:tok + PT], wp_sb[:, a, :],
                                           start=(a == 0), stop=(a == 1))
                    mm.then_inc(pj_full, 1)

            def last(u, half, par):
                pe.wait_ge(av_evac, u)
                norm2_transposes(u - 1)
                mlp_in(u - 1, None)
                for a in range(2):
                    for part in range(3):
                        mlp_out(u - 1, a, part)

            units(pe, step, last)


def build_reorder(nc, scr_a, xs, n_img):
    with ExitStack() as ctx:
        sb = lambda name, shape, dt=F32: ctx.enter_context(nc.sbuf_tensor("b_" + name, shape, dt))
        sem = lambda name: ctx.enter_context(nc.semaphore(name))
        rolled = sb("rolled", [HC, 2, L])
        nat = sb("nat", [HC, 2, L])
        tra = sb("tra", [HC, 2, L])
        r_in = [sem("b_in0"), sem("b_in1")]
        nat_done, tra_done = sem("b_nat_done"), sem("b_tra_done")
        nat_out = [sem("b_nat_out0"), sem("b_nat_out1")]
        tra_out = [sem("b_tra_out0"), sem("b_tra_out1")]
        K = IMG - SHIFT
        pieces = [((0, K), (SHIFT, IMG)), ((K, IMG), (0, SHIFT))]
        fence = sem("reorde_fence")
        block = ctx.enter_context(nc.Block())

        @block.sync
        def _(sp):
            for a in range(2):
                sp.sem_inc(nat_out[a], 16)
                sp.sem_inc(tra_out[a], 16)

            def load(b, a):
                src = scr_a[bass.ds(b * UW, UW), HC * a:HC * a + HC, :].rearrange("u p t -> p u t")
                sp.dma_start(rolled[:, a].rearrange("p (u t) -> p u t", u=UW), src).then_inc(r_in[a], 16)

            def store(b, a, first):
                sp.wait_ge(nat_done, 2 * b + a + 1)
                sp.dma_start(xs[bass.ds(2 * b, 1), a].rearrange("u p t -> p (u t)"), nat[:, a]).then_inc(nat_out[a], 16)
                sp.wait_ge(tra_done, 2 * b + a + 1)
                sp.dma_start(xs[bass.ds(2 * b + 1, 1), a].rearrange("u p t -> p (u t)"), tra[:, a]).then_inc(tra_out[a], 16)

            for a in range(2):
                load(0, a)
            if n_img > 1:
                with sp.Fori(0, n_img - 1) as b:
                    for a in range(2):
                        store(b, a, False)
                        load(b + 1, a)
            for a in range(2):
                store(n_img - 1, a, False)
            for a in range(2):
                sp.wait_ge(nat_out[a], 16 * n_img + 16)
                sp.wait_ge(tra_out[a], 16 * n_img + 16)

        @block.scalar
        def _(act):
            with act.Fori(0, n_img) as b:
                for a in range(2):
                    act.wait_ge(r_in[a], 16 * b + 16)
                    act.wait_ge(nat_out[a], 16 * b + 16)
                    src = rolled[:, a].rearrange("p (h w) -> p h w", h=IMG)
                    dst = nat[:, a].rearrange("p (h w) -> p h w", h=IMG)
                    for (i0, i1), (h0, h1) in pieces:
                        for (j0, j1), (w0, w1) in pieces:
                            ins = nc.scalar.activation(dst[:, h0:h1, w0:w1], src[:, i0:i1, j0:j1], ACT.Copy)
                    ins.then_inc(nat_done, 1)

        @block.vector
        def _(dve):
            with dve.Fori(0, n_img) as b:
                for a in range(2):
                    dve.wait_ge(r_in[a], 16 * b + 16)
                    dve.wait_ge(tra_out[a], 16 * b + 16)
                    src = rolled[:, a].rearrange("p (h w) -> p h w", h=IMG)
                    dst = tra[:, a].rearrange("p (w h) -> p h w", h=IMG)
                    for (i0, i1), (h0, h1) in pieces:
                        for (j0, j1), (w0, w1) in pieces:
                            ins = nc.vector.tensor_copy(dst[:, h0:h1, w0:w1], src[:, i0:i1, j0:j1])
                    ins.then_inc(tra_done, 1)


def build_scan_weights(nc, io, wpk, apk):
    xpT, xpr, dtwT, dtb, a_log = io
    with ExitStack() as ctx:
        sb = lambda name, shape, dt=F32: ctx.enter_context(nc.sbuf_tensor("w_" + name, shape, dt))
        sem = lambda name: ctx.enter_context(nc.semaphore(name))
        ps = ctx.enter_context(nc.psum_tensor("w_psum", [HC, 8, 512], F32))
        xpT_sb = sb("xpT_sb", [HC, 4, 2, RANK + 2 * NS])
        xpr_sb = sb("xpr_sb", [RANK, 4, C])
        dtw_sb = sb("dtw_sb", [RANK, 4, C])
        al_sb = sb("al_sb", [128, 4, NG])
        pack = sb("pack", [HC, 4, WPK])
        w_in, w_mm, w_pk, w_exp, w_neg, w_out = (sem(n) for n in ("w_in", "w_mm", "w_pk", "w_exp", "w_neg", "w_out"))
        fence = sem("scanw_fence")
        block = ctx.enter_context(nc.Block())

        @block.sync
        def _(sp):
            sp.dma_start(xpT_sb[:], xpT).then_inc(w_in, 16)
            sp.dma_start(xpr_sb[:], xpr).then_inc(w_in, 16)
            sp.dma_start(dtw_sb[:], dtwT).then_inc(w_in, 16)
            sp.dma_start(al_sb[:], a_log).then_inc(w_in, 16)
            sp.dma_start(pack[:, :, WPK - 2:WPK], dtb).then_inc(w_in, 16)
            sp.wait_ge(w_in, 80)
            sp.wait_ge(w_pk, 1)
            sp.dma_start(wpk.rearrange("k p w -> p k w"), pack[:]).then_inc(w_out, 16)
            sp.wait_ge(w_neg, 1)
            sp.dma_start(apk.rearrange("k p g -> p k g"), al_sb[:]).then_inc(w_out, 16)
            sp.wait_ge(w_out, 32)

        @block.tensor
        def _(pe):
            pe.wait_ge(w_in, 80)
            for k in range(4):
                for a in range(2):
                    mm = pe.matmul(ps[:, 2 * k + a, 0:C], xpr_sb[:, k, HC * a:HC * a + HC], dtw_sb[:, k, :],
                                   start=True, stop=True)
            mm.then_inc(w_mm, 1)

        @block.vector
        def _(dve):
            dve.wait_ge(w_in, 80)
            for k in range(4):
                for m in range(2):
                    for a in range(2):
                        src = xpT_sb[:, k, a, RANK + NS * m:RANK + NS * m + NS].unsqueeze(2).to_broadcast([HC, NS, DG])
                        o = 2 * C + 256 * m + 128 * a
                        nc.vector.tensor_copy(pack[:, k, o:o + 128].rearrange("p (n d) -> p n d", d=DG), src)
            dve.wait_ge(w_mm, 1)
            for k in range(4):
                ins = nc.vector.tensor_copy(pack[:, k, 0:2 * C].rearrange("p (a d) -> p a d", a=2), ps[:, 2 * k:2 * k + 2, 0:C])
            ins.then_inc(w_pk, 1)
            dve.wait_ge(w_exp, 1)
            nc.vector.tensor_scalar(al_sb[:], al_sb[:], -1.0, None, ALU.mult).then_inc(w_neg, 1)

        @block.scalar
        def _(act):
            act.wait_ge(w_in, 80)
            nc.scalar.activation(al_sb[:], al_sb[:], ACT.Exp).then_inc(w_exp, 1)


def build_scan(nc, io, xs, wpk, apk, ysc, n_img):
    sel_h, red_h = io
    NSTEP = NG
    RA, RB, RH, RP = 4, 3, 4, 8
    NV = n_img * 2 * NCH * 2
    with ExitStack() as ctx:
        sb = lambda name, shape, dt=F32: ctx.enter_context(nc.sbuf_tensor("c_" + name, shape, dt))
        sem = lambda name: ctx.enter_context(nc.semaphore(name))
        ps = ctx.enter_context(nc.psum_tensor("c_psum", [128, 4096], F32))
        HT = CH // 2
        DH = [ps[:, 0:HT], ps[:, 512:512 + HT]]
        U = [ps[:, 1024:1024 + CH], ps[:, 2048:2048 + CH]]
        Y = [ps[0:HC, 3072:3072 + HT], ps[0:HC, 3584:3584 + HT]]
        cuts = [(0, 512), (512, CH)]

        sel_f = sb("sel_f", [96, 4, 128])
        sel = sb("sel", [96, 4, 128], BF16)
        red = sb("red", [128, 4, 32])
        zero = sb("zero", [128, NG])
        one = sb("one", [HC, 1])
        x_u = sb("x_u", [HC, 2, 2, CH])
        w_u = sb("w_u", [HC, 2, WPK])
        a_u = sb("a_u", [128, 2, NG])
        init = sb("init", [128, 2, NG])
        lastc = sb("lastc", [128, 2, NG])
        bc = sb("bc", [128, 2, 2, CH])
        pk = sb("pk", [96, 2, 2, NQ, CH], BF16)
        e_t = sb("e_t", [HC, CH])
        rl_t = sb("rl_t", [HC, CH])
        l_t = sb("l_t", [HC, CH])
        w_t = sb("w_t", [HC, CH])
        du = sb("du", [HC, 2, CH])
        rem = sb("rem", [HC, 2, CH])
        parts = sb("parts", [HC, 2, 2, 3, CH], BF16)
        dA = sb("dA", [128, RA, CH])
        dbx = sb("dbx", [128, RB, CH])
        hs = sb("hs", [128, RH, CH])
        pr = sb("pr", [128, RP, CH])
        y_sb = sb("y_sb", [HC, 2, CH])

        const_in = sem("c_const")
        one_done = sem("c_one")
        sel_done = sem("c_sel")
        xw_in = [sem("c_xw_in0"), sem("c_xw_in1")]
        ai_in = [sem("c_ai_in0"), sem("c_ai_in1")]
        d_full, exp_done = sem("c_d_full"), sem("c_exp_done")
        u_full, mul_done, scan_done = sem("c_u_full"), sem("c_mul_done"), sem("c_scan_done")
        carry_done = sem("c_carry_done")
        prod_done = sem("c_prod_done")
        y_evac = sem("c_y_evac")
        y_out = [sem("c_y_out0"), sem("c_y_out1")]
        raw_full, raw_evac = sem("c_raw_full"), sem("c_raw_evac")
        act_sp = sem("c_act_sp")
        dve_sp = sem("c_dve_sp")
        dt_done = sem("c_dt_done")
        u_done = sem("c_u_done")
        hi_done, rem_done = sem("c_hi_done"), sem("c_rem_done")
        mid_done, lo_done = sem("c_mid_done"), sem("c_lo_done")
        pk_in = [[sem(f"c_pk_in{d}{a}") for a in range(2)] for d in range(2)]
        red_done = sem("c_red_done")
        N_PK = 16 * 9
        WI = 2 * NCH * 2
        DT, MAT_B, MAT_C = (0, 1), 2, 3
        ITEMS = [(k, t) for k in (DT[0], MAT_B, DT[1], MAT_C) for t in range(2)]
        ITEM_AT = {1: 0, 3: 1, 5: 2, 7: 3, 9: 4, 11: 5, 16: 6, 20: 7}
        DT_ITEMS = (2, 6)
        B_ITEMS = 4
        EXP_AT, LOG_AT = (4, 12), (5, 13)
        SP1_AT, SP2_AT = (3, 11), (5, 12)
        U_AT = (5, 14)
        HI_AT = {9: (0, 0), 11: (0, 1), 17: (1, 0), 20: (1, 1)}
        REM_AT = {9: (0, 0), 10: (0, 1), 16: (1, 0), 18: (1, 1)}
        MID_AT = {12: (0, 0), 15: (0, 1), 20: (1, 0), 23: (1, 1)}
        LO_AT = {8: (0, 0), 11: (0, 1), 22: (1, 0), 23: (1, 1)}
        LEAD = 2
        RED_LAG = 8
        EVAC_AT = {(12 * (a + 1) + RED_LAG + t) % NG: (a, t) for a in range(2) for t in range(2)}

        fence = sem("scan_fence")
        block = ctx.enter_context(nc.Block())

        def step_ids(s):
            hh, j, qq = s // 12, (s % 12) // 3, s % 3
            return hh, j, qq, 4 * (3 * hh + qq) + j

        @block.sync
        def _(sp):
            sp.dma_start(sel_f[:], sel_h).then_inc(const_in, 16)
            sp.dma_start(red[:], red_h).then_inc(const_in, 16)
            for a in range(2):
                sp.sem_inc(y_out[a], 16)

            def unit_of(w):
                o, c, d = w // (2 * NCH), w // 2 % NCH, w % 2
                return o, (c if d == 0 else NCH - 1 - c), d

            def load_xw(b, w):
                o, cc, d = unit_of(w)
                sp.dma_start(x_u[:, d], xs[bass.ds(2 * b + o, 1), :, :, CH * cc:CH * cc + CH].rearrange(
                    "u a p t -> p (u a) t")).then_inc(xw_in[d], 16)
                sp.dma_start(w_u[:, d], wpk[o + 2 * d]).then_inc(xw_in[d], 16)

            def load_ai(w):
                o, _, d = unit_of(w)
                sp.dma_start(a_u[:, d], apk[o + 2 * d]).then_inc(ai_in[d], 16)
                starts = w % (2 * NCH) < 2
                sp.dma_start(init[:, d], zero[:] if starts else lastc[:, d]).then_inc(ai_in[d], 16)

            def packs(v, w, a):
                d = w % 2
                sp.wait_ge(lo_done, 4 * v + 2 * a + 2)
                for k in range(3):
                    for q in range(3):
                        sp.dma_start(pk[32 * k:32 * k + 32, d, :, 3 * a + q, :],
                                     parts[32 * q:32 * q + 32, a, :, k, :]).then_inc(pk_in[d][a], 16)

            def store_y(b, v, w, a):
                o, cc, d = unit_of(w)
                sp.wait_ge(y_evac, 4 * v + 2 * a + 2)
                sp.dma_start(ysc[bass.ds(2 * b + o, 1), d, a, :, CH * cc:CH * cc + CH].rearrange("u p t -> (u p) t"),
                             y_sb[:, a]).then_inc(y_out[a], 16)

            def window(b, w, final):
                v = WI * b + w
                more1, more2 = not (final and w + 1 >= WI), not (final and w + 2 >= WI)
                if more2:
                    hold(sp, raw_evac, 8 * v + 8, fence)
                    hold(sp, u_done, 2 * v + 2, fence)
                    load_xw(b + (w + 2) // WI, (w + 2) % WI)
                if more1:
                    packs(v + 1, (w + 1) % WI, 0)
                store_y(b, v, w, 0)
                if more1:
                    packs(v + 1, (w + 1) % WI, 1)
                if more2:
                    hold(sp, exp_done, 2 * NSTEP * (v + 1), fence)
                    hold(sp, scan_done, NSTEP * (v + 1), fence)
                    hold(sp, carry_done, NSTEP // RH * (v + 1), fence)
                    load_ai((w + 2) % WI)
                store_y(b, v, w, 1)

            sp.wait_ge(one_done, 1)
            for w in range(2):
                load_xw(0, w)
                load_ai(w)
            packs(0, 0, 0)
            packs(0, 0, 1)
            if n_img > 1:
                with sp.Fori(0, n_img - 1) as b:
                    for w in range(WI):
                        window(b, w, False)
            for w in range(WI):
                window(n_img - 1, w, True)
            for a in range(2):
                sp.wait_ge(y_out[a], 16 * NV + 16)

        def all_units(eng, unit):
            unit(0, 0, 0, True, False)
            with eng.Fori(0, NV // 2 - 1) as i:
                unit(2 * i + 1, i, 1, False, False)
                unit(2 * i + 2, i + 1, 0, False, False)
            unit(NV - 1, NV // 2 - 1, 1, False, True)

        @block.tensor
        def _(pe):
            pe.wait_ge(const_in, 32)
            pe.wait_ge(sel_done, 1)

            def prepare(v, h, d, i):
                k, t = ITEMS[i]
                if i == 0:
                    pe.wait_ge(xw_in[d], 32 * h + 32)
                for a in range(2):
                    o = C * a + HC * k if k < 2 else 2 * C + 256 * (k - 2) + 128 * a
                    n = HC if k < 2 else 128
                    mm = pe.matmul(DH[t][0:n, :], w_u[:, d, o:o + n], x_u[:, d, a, HT * t:HT * t + HT],
                                   start=(a == 0), stop=(a == 1))
                mm.then_inc(raw_full, 1)

            def reduce(v, n):
                m = n // 3
                for piece in (2 * (n % 3), 2 * (n % 3) + 1):
                    t, qq = piece // 3, piece % 3
                    if qq == 0 and m % 4 == 0 and not (isinstance(v, int) and v == 0 and m == 0):
                        pe.wait_ge(y_evac, 4 * v + 2 * (m // 4) - 1 + t)
                    if piece == 0:
                        pe.wait_ge(prod_done, NSTEP * v + 3 * m + 3)
                    mm = pe.matmul(Y[t][32 * qq:32 * qq + 32, :], red[:, m % 4, :],
                                   pr[:, (3 * m + qq) % RP, HT * t:HT * t + HT], start=(m % 4 == 0), stop=(m % 4 == 3))
                    if qq == 2:
                        mm.then_inc(red_done, 1)

            def spread_dt(v, h, d, s, first, item):
                hh, j, qq, _ = step_ids(s)
                for t in range(2):
                    if item is not None and ITEMS[item][1] == t:
                        pe.wait_ge(raw_evac, 8 * v + 8 + item + 1)
                    elif first and s == 0:
                        pe.wait_ge(raw_evac, 7 + t)
                    else:
                        pe.wait_ge(exp_done, 2 * (NSTEP * v + s) - 1 + t)
                    if s % 12 == 0 and t == 0:
                        pe.wait_ge(pk_in[d][hh], N_PK * h + N_PK)
                    pe.matmul(DH[t], sel[:, j, :], pk[:, d, 0, 3 * hh + qq, HT * t:HT * t + HT],
                              start=True, stop=True).then_inc(d_full, 1)

            for i in range(len(ITEMS)):
                if i >= 2:
                    pe.wait_ge(raw_evac, i - 1)
                prepare(0, 0, 0, i)
            for s in range(LEAD):
                spread_dt(0, 0, 0, s, True, None)

            def unit(v, h, d, first, last):
                for s in range(NSTEP):
                    hh, j, qq, _ = step_ids(s)
                    if not (first and s < 2):
                        pe.wait_ge(mul_done, NSTEP * v + s - 1)
                    for n0, n1 in cuts:
                        mm = pe.matmul(U[s % 2][:, n0:n1], sel[:, j, :], pk[:, d, 1, 3 * hh + qq, n0:n1],
                                       start=True, stop=True)
                    mm.then_inc(u_full, 1)
                    ahead = s + LEAD
                    if ahead - 1 in ITEM_AT and not last:
                        item = ITEM_AT[ahead - 1]
                        pe.wait_ge(exp_done, 2 * (NSTEP * v + ahead - 1) + 1 + ITEMS[item][1])
                        prepare(v + 1, h + d, 1 - d, item)
                    if s >= RED_LAG:
                        reduce(v, s - RED_LAG)
                    elif not first:
                        reduce(v - 1, s + NSTEP - RED_LAG)
                    if ahead < NSTEP:
                        spread_dt(v, h, d, ahead, first, None if last else ITEM_AT.get(ahead - 1))
                    elif not last:
                        spread_dt(v + 1, h + d, 1 - d, ahead - NSTEP, False, None)
                if last:
                    for n in range(NSTEP - RED_LAG, NSTEP):
                        reduce(v, n)

            all_units(pe, unit)

        @block.scalar
        def _(act):
            def item(v, h, d, i, start):
                k, t = ITEMS[i]
                now = slice(HT * t, HT * t + HT)
                act.wait_ge(raw_full, 8 * v + i + 1)
                if k < 2:
                    bias = w_u[:, d, WPK - 2 + k:WPK - 1 + k]
                    if t == 0 and not (start and k == 0):
                        act.wait_ge(dt_done, 2 * v + k)
                    nc.scalar.activation(e_t[:, now], DH[t][0:HC, :], ACT.Abs, bias=bias).then_inc(act_sp, 1)
                    nc.scalar.activation(rl_t[:, now], DH[t][0:HC, :], ACT.Relu, bias=bias).then_inc(raw_evac, 1)
                else:
                    if t == 0 and not start:
                        act.wait_ge(prod_done, NSTEP * (v - 1))
                    nc.scalar.activation(bc[:, d, k - 2, now], DH[t], ACT.Copy).then_inc(raw_evac, 1)

            def exponential(v, a):
                n = 10 * v + 5 * a
                act.wait_ge(act_sp, n + 2)
                nc.scalar.activation(e_t[:], e_t[:], ACT.Exp, scale=-1.0).then_inc(act_sp, 1)

            def logarithm(v, a):
                n = 10 * v + 5 * a
                act.wait_ge(act_sp, n + 3)
                nc.scalar.activation(w_t[:], e_t[:], ACT.Identity, bias=one[:, 0:1]).then_inc(act_sp, 1)
                act.wait_ge(act_sp, n + 4)
                nc.scalar.activation(l_t[:], w_t[:], ACT.Ln).then_inc(act_sp, 1)

            def high(v, h, d, a, m, start):
                if m == 0:
                    act.wait_ge(dt_done, 2 * v + a + 1)
                    if not start:
                        act.wait_ge(pk_in[1 - d][a], N_PK * h + N_PK * d)
                else:
                    act.wait_ge(u_done, 2 * v + a + 1)
                nc.scalar.activation(parts[:, a, m, 0, :], du[:, m, :], ACT.Copy).then_inc(hi_done, 1)

            def middle(v, a, m):
                act.wait_ge(rem_done, 4 * v + 2 * a + m + 1)
                nc.scalar.activation(parts[:, a, m, 1, :], rem[:, m, :], ACT.Copy).then_inc(mid_done, 1)

            def evacuate(v, a, t):
                act.wait_ge(red_done, 16 * v + 8 * a + 7 + t)
                if t == 0:
                    act.wait_ge(y_out[a], 16 * v + 16)
                nc.scalar.activation(y_sb[:, a, HT * t:HT * t + HT], Y[t], ACT.Copy).then_inc(y_evac, 1)

            act.wait_ge(const_in, 32)
            nc.scalar.activation(sel[:], sel_f[:], ACT.Copy).then_inc(sel_done, 1)
            nc.scalar.preload_act_table_set(LN_EXP)
            act.wait_ge(one_done, 1)
            act.wait_ge(xw_in[0], 32)
            for a in range(2):
                for i in range(4 * a, 4 * a + 4 - 2 * a):
                    item(0, 0, 0, i, True)
                exponential(0, a)
                logarithm(0, a)
                for m in range(2):
                    high(0, 0, 0, a, m, True)
                for m in range(2):
                    middle(0, a, m)
            for i in range(6, 8):
                item(0, 0, 0, i, True)

            def unit(v, h, d, first, last):
                act.wait_ge(ai_in[d], 32 * h + 32)
                nh, nd = h + d, 1 - d
                for s in range(NSTEP):
                    col = step_ids(s)[3]
                    if not (first and s < RA):
                        act.wait_ge(scan_done, NSTEP * v + s + 1 - RA)
                    for t in range(2):
                        act.wait_ge(d_full, 2 * (NSTEP * v + s) + t + 1)
                        nc.scalar.activation(dA[:, s % RA, HT * t:HT * t + HT], DH[t], ACT.Exp,
                                             scale=a_u[:, d, col:col + 1]).then_inc(exp_done, 1)
                    if not last:
                        if s == 0:
                            act.wait_ge(xw_in[nd], 32 * nh + 32)
                        if s in EXP_AT:
                            exponential(v + 1, EXP_AT.index(s))
                        if s in LOG_AT:
                            logarithm(v + 1, LOG_AT.index(s))
                        if s in HI_AT:
                            high(v + 1, nh, nd, *HI_AT[s], False)
                        if s in MID_AT:
                            middle(v + 1, *MID_AT[s])
                    if s in EVAC_AT:
                        a, t = EVAC_AT[s]
                        if a == 0:
                            evacuate(v, 0, t)
                        elif not first:
                            evacuate(v - 1, 1, t)
                    if s in ITEM_AT and not last:
                        item(v + 1, nh, nd, ITEM_AT[s], first and ITEMS[ITEM_AT[s]][0] not in DT)
                if last:
                    evacuate(v, 1, 0)
                    evacuate(v, 1, 1)

            all_units(act, unit)

        @block.vector
        def _(dve):
            nc.vector.memset(one[:], 1.0)
            nc.vector.memset(zero[:], 0.0).then_inc(one_done, 1)

            def softplus1(v, a):
                k = 2 * v + a
                dve.wait_ge(act_sp, 5 * k + 5)
                nc.vector.scalar_tensor_tensor(l_t[:], w_t[:], -1.0, l_t[:], ALU.add, ALU.min)
                nc.vector.scalar_tensor_tensor(w_t[:], w_t[:], -1.0, e_t[:], ALU.add, ALU.subtract).then_inc(dve_sp, 1)

            def softplus2(v, a, start):
                k = 2 * v + a
                dve.wait_ge(dve_sp, 2 * k + 1)
                nc.vector.tensor_tensor(w_t[:], l_t[:], w_t[:], ALU.subtract).then_inc(dve_sp, 1)
                dve.wait_ge(dve_sp, 2 * k + 2)
                dve.wait_ge(raw_evac, 8 * v + DT_ITEMS[a])
                if not (start and a == 0):
                    dve.wait_ge(hi_done, 2 * k)
                    dve.wait_ge(u_done, k)
                nc.vector.tensor_tensor(du[:, 0, :], w_t[:], rl_t[:], ALU.add).then_inc(dt_done, 1)

            def remainder(v, a, m, start):
                dve.wait_ge(hi_done, 4 * v + 2 * a + m + 1)
                if not (start and a == 0):
                    dve.wait_ge(lo_done, 4 * v + 2 * a)
                nc.vector.tensor_tensor(rem[:, m, :], du[:, m, :], parts[:, a, m, 0, :], ALU.subtract).then_inc(rem_done, 1)

            for a in range(2):
                softplus1(0, a)
                softplus2(0, a, True)
                remainder(0, a, 0, True)
                remainder(0, a, 1, True)

            def keep_states(v, d, s):
                col = CH - 1 if d == 0 else 0
                dve.wait_ge(scan_done, NSTEP * v + s)
                nc.vector.tensor_copy(lastc[:, d, s - RH:s], hs[:, :, col]).then_inc(carry_done, 1)

            def times_b(v, d, s, first):
                n = NSTEP * v + s
                if s == 0:
                    dve.wait_ge(raw_evac, 8 * v + B_ITEMS)
                dve.wait_ge(u_full, n + 1)
                if not (first and s < RB):
                    dve.wait_ge(scan_done, n + 1 - RB)
                nc.vector.tensor_tensor(dbx[:, s % RB, :], U[s % 2], bc[:, d, 0, :], ALU.mult).then_inc(mul_done, 1)

            times_b(0, 0, 0, True)

            def unit(v, h, d, first, last):
                way = slice(None, None, 1 if d == 0 else -1)
                for s in range(NSTEP):
                    n = NSTEP * v + s
                    if s + 1 < NSTEP:
                        times_b(v, d, s + 1, first)
                    elif not last:
                        times_b(v + 1, 1 - d, 0, False)
                    if s and s % RH == 0:
                        keep_states(v, d, s)
                    elif s == 0 and not first:
                        keep_states(v - 1, 1 - d, NSTEP)
                    if s == 0:
                        dve.wait_ge(ai_in[d], 32 * h + 32)
                    dve.wait_ge(exp_done, 2 * n + 2)
                    dve.wait_ge(mul_done, n + 1)
                    if not (first and s < RH):
                        dve.wait_ge(prod_done, n + 1 - RH)
                    if s % RH == 0 and not (first and s == 0):
                        dve.wait_ge(carry_done, NSTEP // RH * v + s // RH)
                    nc.vector.tensor_tensor_scan(hs[:, s % RH, way], dA[:, s % RA, way], dbx[:, s % RB, way],
                                                 init[:, d, s:s + 1], ALU.mult, ALU.add).then_inc(scan_done, 1)
                    if not last:
                        if s in SP1_AT:
                            softplus1(v + 1, SP1_AT.index(s))
                        if s in REM_AT:
                            remainder(v + 1, *REM_AT[s], False)
                        if s in SP2_AT:
                            softplus2(v + 1, SP2_AT.index(s), False)

            all_units(dve, unit)

        @block.gpsimd
        def _(pool):
            def dt_x(v, h, d, a, start):
                pool.wait_ge(dt_done, 2 * v + a + 1)
                if a == 0:
                    pool.wait_ge(xw_in[d], 32 * h + 32)
                if not (start and a == 0):
                    pool.wait_ge(rem_done, 4 * v + 2 * a)
                nc.gpsimd.tensor_tensor(du[:, 1, :], du[:, 0, :], x_u[:, d, a, :], ALU.mult).then_inc(u_done, 1)

            def low(v, a, m):
                pool.wait_ge(mid_done, 4 * v + 2 * a + m + 1)
                nc.gpsimd.tensor_tensor(parts[:, a, m, 2, :], rem[:, m, :], parts[:, a, m, 1, :],
                                        ALU.subtract).then_inc(lo_done, 1)

            for a in range(2):
                dt_x(0, 0, 0, a, True)
                low(0, a, 0)
                low(0, a, 1)

            def unit(v, h, d, first, last):
                pool.wait_ge(raw_evac, 8 * v + 8)
                for s in range(NSTEP):
                    pool.wait_ge(scan_done, NSTEP * v + s + 1)
                    if not (first and s < RP):
                        pool.wait_ge(red_done, 16 * v + 2 * ((s - RP) // 3) + 2)
                    nc.gpsimd.tensor_tensor(pr[:, s % RP, :], hs[:, s % RH, :], bc[:, d, 1, :], ALU.mult).then_inc(prod_done, 1)
                    if not last:
                        if s in U_AT:
                            dt_x(v + 1, h + d, 1 - d, U_AT.index(s), False)
                        if s in LO_AT:
                            low(v + 1, *LO_AT[s])

            all_units(pool, unit)


def build_output(nc, io, xs, ysc, out, n_img):
    ds_h, lnw, lnb, ident = io
    NGRP = NT // GT
    with ExitStack() as ctx:
        sb = lambda name, shape, dt=F32: ctx.enter_context(nc.sbuf_tensor("d_" + name, shape, dt))
        sem = lambda name: ctx.enter_context(nc.semaphore(name))
        ps = ctx.enter_context(nc.psum_tensor("d_psum", [TT, 8, 512], F32))
        yin = sb("yin", [HC, 2, 4, L])
        x_in = sb("x_in", [HC, 2, L])
        yf = sb("yf", [HC, 2, L])
        ds_sb = sb("ds_sb", [HC, 2, 4])
        dsum = sb("dsum", [HC, 2])
        w_sb = sb("w_sb", [TT, C])
        b_sb = sb("b_sb", [TT, C])
        id_sb = sb("id_sb", [HC, HC])
        eps_sb = sb("eps_sb", [TT, 1])
        stats = sb("stats", [TT, 2, GT, 6])
        mv = sb("mv", [TT, NGRP, GT, 2])
        lnv = sb("lnv", [TT, NGRP, GT])
        rstd = sb("rstd", [TT, NGRP, GT])
        ob = sb("ob", [TT, NGRP, GT * C])
        c_in = sem("d_c_in")
        y_in = [sem("d_y_in0"), sem("d_y_in1")]
        ready = sem("d_ready")
        row_done, col_done, add_done, yf_done = sem("d_row"), sem("d_col"), sem("d_add"), sem("d_yf")
        t_full, st_done, ag_done = sem("d_t_full"), sem("d_st"), sem("d_ag")
        ln_done, rs_done, nm_done = sem("d_ln"), sem("d_rs"), sem("d_nm")
        wm_done, o_done = sem("d_wm"), sem("d_o")
        o_out = [sem(f"d_o_out{g}") for g in range(NGRP)]
        tile_ps = lambda g, t: ps[:, 2 * (g % 4) + t // 2, C * (t % 2):C * (t % 2) + C]
        fence = sem("output_fence")
        block = ctx.enter_context(nc.Block())

        @block.sync
        def _(sp):
            for dst, src in ((ds_sb[:], ds_h), (id_sb[:], ident[0:HC, 0:HC]),
                             (w_sb[:], lnw.unsqueeze(0).to_broadcast([TT, C])),
                             (b_sb[:], lnb.unsqueeze(0).to_broadcast([TT, C]))):
                sp.dma_start(dst, src).then_inc(c_in, 16)

            def load(b, a):
                for o in range(2):
                    sp.dma_start(yin[:, a, 2 * o:2 * o + 2, :],
                                 ysc[bass.ds(2 * b + o, 1), :, a].rearrange("u d p t -> p (u d) t")).then_inc(y_in[a], 16)
                sp.dma_start(x_in[:, a], xs[bass.ds(2 * b, 1), a].rearrange("u p t -> p (u t)")).then_inc(y_in[a], 16)

            def stores(b):
                for g in range(NGRP):
                    sp.wait_ge(o_done, NGRP * b + g + 1)
                    dst = out[bass.ds(b, 1), TT * GT * g:TT * GT * (g + 1), :].rearrange("u (t p) c -> p (u t) c", p=TT)
                    sp.dma_start(dst, ob[:, g].rearrange("p (t c) -> p t c", t=GT)).then_inc(o_out[g], 16)

            load(0, 0)
            load(0, 1)
            if n_img > 1:
                with sp.Fori(0, n_img - 1) as b:
                    for a in range(2):
                        sp.wait_ge(yf_done, 2 * b + a + 1)
                        load(b + 1, a)
                    stores(b)
            stores(n_img - 1)
            for g in range(NGRP):
                sp.wait_ge(o_out[g], 16 * n_img + 16)

        def images(eng, body):
            body(0, True)
            if n_img > 1:
                with eng.Fori(1, n_img) as b:
                    body(b, False)

        @block.gpsimd
        def _(pool):
            pool.wait_ge(c_in, 64)
            for g in range(NGRP):
                pool.sem_inc(o_out[g], 16)

            def body(b, first):
                for a in range(2):
                    pool.wait_ge(y_in[a], 48 * b + 48)
                    nc.gpsimd.tensor_tensor(yin[:, a, 2], yin[:, a, 2], yin[:, a, 3], ALU.add).then_inc(col_done, 1)
                for g in range(NGRP):
                    n = NGRP * b + g
                    pool.wait_ge(nm_done, n + 1)
                    o = ob[:, g].rearrange("p (t c) -> p t c", t=GT)
                    nc.gpsimd.tensor_tensor(o, o, w_sb[:].unsqueeze(1).to_broadcast([TT, GT, C]), ALU.mult).then_inc(wm_done, 1)
                    pool.wait_ge(wm_done, n + 1)
                    nc.gpsimd.tensor_tensor(o, o, b_sb[:].unsqueeze(1).to_broadcast([TT, GT, C]), ALU.add).then_inc(o_done, 1)

            images(pool, body)

        @block.vector
        def _(dve):
            nc.vector.memset(eps_sb[:], LN_EPS).then_inc(ready, 1)
            dve.wait_ge(c_in, 64)
            nc.vector.tensor_reduce(dsum[:], ds_sb[:], AX_X, ALU.add).then_inc(ready, 1)
            dve.wait_ge(ready, 2)

            def body(b, first):
                for a in range(2):
                    n = 2 * b + a
                    dve.wait_ge(y_in[a], 48 * b + 48)
                    nc.vector.tensor_tensor(yin[:, a, 0], yin[:, a, 0], yin[:, a, 1], ALU.add).then_inc(row_done, 1)
                    dve.wait_ge(row_done, n + 1)
                    dve.wait_ge(col_done, n + 1)
                    sq = lambda ap, p: ap.rearrange(p, h=IMG)
                    nc.vector.tensor_tensor(sq(yin[:, a, 0], "p (h w) -> p h w"), sq(yin[:, a, 0], "p (h w) -> p h w"),
                                            sq(yin[:, a, 2], "p (w h) -> p h w"), ALU.add).then_inc(add_done, 1)
                    dve.wait_ge(add_done, n + 1)
                    if a == 0 and not first:
                        dve.wait_ge(t_full, NGRP * b)
                    nc.vector.scalar_tensor_tensor(yf[:, a], x_in[:, a], dsum[:, a:a + 1], yin[:, a, 0],
                                                   ALU.mult, ALU.add).then_inc(yf_done, 1)

                def stat(g):
                    n = NGRP * b + g
                    dve.wait_ge(t_full, n + 1)
                    for t in range(GT):
                        ins = nc.vector.bn_stats(stats[:, g % 2, t], tile_ps(g, t))
                    ins.then_inc(st_done, 1)
                    if g == 0 and not first:
                        dve.wait_ge(rs_done, NGRP * b)
                    hold(dve, st_done, n + 1, fence)
                    for t in range(GT):
                        ins = nc.vector.bn_aggr(mv[:, g, t], stats[:, g % 2, t])
                    ins.then_inc(ag_done, 1)

                def normalise(g):
                    n = NGRP * b + g
                    dve.wait_ge(rs_done, n + 1)
                    dve.wait_ge(o_out[g], 16 * b + 16)
                    for t in range(GT):
                        ins = nc.vector.tensor_scalar(ob[:, g, C * t:C * t + C], tile_ps(g, t), mv[:, g, t, 0:1],
                                                      rstd[:, g, t:t + 1], ALU.subtract, ALU.mult)
                    ins.then_inc(nm_done, 1)

                for g in range(NGRP):
                    stat(g)
                    if g:
                        normalise(g - 1)
                normalise(NGRP - 1)

            images(dve, body)

        @block.scalar
        def _(act):
            act.wait_ge(ready, 1)
            nc.scalar.preload_act_table_set(LN_EXP)

            def body(b, first):
                for g in range(NGRP):
                    n = NGRP * b + g
                    act.wait_ge(ag_done, n + 1)
                    nc.scalar.activation(lnv[:, g], mv[:, g, :, 1], ACT.Ln, bias=eps_sb[:, 0:1]).then_inc(ln_done, 1)
                    act.wait_ge(ln_done, n + 1)
                    if g == 0 and not first:
                        act.wait_ge(nm_done, NGRP * b)
                    nc.scalar.activation(rstd[:, g], lnv[:, g], ACT.Exp, scale=-0.5).then_inc(rs_done, 1)

            images(act, body)

        @block.tensor
        def _(pe):
            pe.wait_ge(c_in, 64)

            def body(b, first):
                pe.wait_ge(yf_done, 2 * b + 2)
                for g in range(NGRP):
                    n = NGRP * b + g
                    if g >= 4:
                        pe.wait_ge(nm_done, n - 3)
                    elif not first and g < 4:
                        pe.wait_ge(nm_done, NGRP * b)
                    for t in range(GT):
                        for a in range(2):
                            tok = TT * (GT * g + t)
                            mm = pe.transpose(tile_ps(g, t)[:, HC * a:HC * a + HC], yf[:, a, tok:tok + TT], id_sb[:])
                    mm.then_inc(t_full, 1)

            images(pe, body)


def build(nc, ins, out, n_img):
    n_units = n_img * UW
    scr_a = nc.dram_tensor("scr_layer0", (n_units, C, UT), F32, kind="Internal").ap()
    xs = nc.dram_tensor("scr_x", (2 * n_img, 2, HC, L), F32, kind="Internal").ap()
    ysc = nc.dram_tensor("scr_y", (2 * n_img, 2, 2, HC, L), F32, kind="Internal").ap()
    wpk = nc.dram_tensor("scr_w", (4, HC, WPK), F32, kind="Internal").ap()
    apk = nc.dram_tensor("scr_a_neg", (4, 128, NG), F32, kind="Internal").ap()
    i = ins
    build_layer0(nc, (i["x_win"], i["qkv_w"], i["proj_w"], i["w1"], i["w2"], i["cols0"], i["b1c"], i["proj_b"],
                      i["ident"]), scr_a, n_units)
    build_reorder(nc, scr_a, xs, n_img)
    build_scan_weights(nc, (i["xpT"], i["xpr"], i["dtwT"], i["dtb"], i["a_log"]), wpk, apk)
    build_scan(nc, (i["sel"], i["red"]), xs, wpk, apk, ysc, n_img)
    build_output(nc, (i["ds"], i["ln_w"], i["ln_b"], i["ident"]), xs, ysc, out, n_img)


def lay_out(inputs):
    import numpy as np
    g = lambda n: np.asarray(inputs[n])
    x = g("x")
    n_img = x.shape[0]
    xw = np.roll(x, (-SHIFT, -SHIFT), axis=(1, 2)).reshape(n_img, UW, WS, UW, WS, C).transpose(0, 1, 3, 2, 4, 5)
    halves = lambda v: v.reshape(-1, HC).T
    cols0 = np.concatenate([halves(g("L0_conv_" + n)) for n in
                            ("ln1_w", "ln1_b", "qkv_b", "ln2_w", "ln2_b", "mlp_b2")], axis=1)
    xp, dtw, dtb = g("L1_conv_x_proj_weight"), g("L1_conv_dt_projs_weight"), g("L1_conv_dt_projs_bias")
    eye = np.eye(128, dtype=np.float32)
    sel = np.zeros((3, 4, DG, 4, NS, DG), np.float32)
    red = np.zeros((NS, DG, 4, 4, DG), np.float32)
    for j in range(4):
        for d in range(DG):
            sel[:, j, d, j, :, d] = 1
            red[:, d, j, j, d] = 1
    return {
        "x_win": xw.reshape(-1, C),
        "qkv_w": g("L0_conv_qkv_w"), "proj_w": g("L0_conv_proj_w"), "w1": g("L0_conv_mlp_w1"), "w2": g("L0_conv_mlp_w2"),
        "cols0": cols0, "b1c": g("L0_conv_mlp_b1").reshape(MC, 128).T, "proj_b": g("L0_conv_proj_b"), "ident": eye,
        "xpT": xp.reshape(4, RANK + 2 * NS, 2, HC).transpose(3, 0, 2, 1),
        "xpr": xp[:, :RANK].transpose(1, 0, 2), "dtwT": dtw.transpose(2, 0, 1),
        "dtb": dtb.reshape(4, 2, HC).transpose(2, 0, 1),
        "a_log": g("L1_conv_A_logs").reshape(4, NG, DG, NS).transpose(3, 2, 0, 1).reshape(128, 4, NG),
        "sel": sel.reshape(96, 4, 128), "red": red.reshape(128, 4, 32),
        "ds": g("L1_conv_Ds").reshape(4, 2, HC).transpose(2, 1, 0),
        "ln_w": g("L1_conv_ln_weight"), "ln_b": g("L1_conv_ln_bias"),
    }


def program(nc, arrays, n_img):
    import numpy as np
    ins = {n: nc.dram_tensor(f"in_{n}", a.shape, mybir.dt.from_np(a.dtype), kind="ExternalInput").ap()
           for n, a in arrays.items()}
    out = nc.dram_tensor("out", (n_img, L, C), F32, kind="ExternalOutput").ap()
    build(nc, ins, out, n_img)


def kernel(**inputs):
    import numpy as np
    from concourse import bacc
    from concourse.bass_utils import run_bass_kernel_spmd
    arrays = {n: np.ascontiguousarray(a) for n, a in lay_out(inputs).items()}
    n_img = np.asarray(inputs["x"]).shape[0]
    nc = bacc.Bacc("TRN2", target_bir_lowering=False, num_devices=1)
    program(nc, arrays, n_img)
    r = run_bass_kernel_spmd(nc, [{f"in_{n}": a for n, a in arrays.items()}], core_ids=[0])
    return r.results[0]["out"].reshape(n_img, IMG, IMG, C)
```
